# Optimizing a Trainium2 kernel written in Bass

```python
import numpy as np
import jax
import jax.numpy as jnp

def _softmax(x, axis=-1):
    return jax.nn.softmax(x, axis=axis)

def _gelu(x):
    return jax.nn.gelu(x, approximate=True)

def _silu(x):
    return jax.nn.silu(x)

def _sigmoid(x):
    return jax.nn.sigmoid(x)

def _layernorm(x, axis=-1, eps=1e-05):
    m = jnp.mean(x, axis=axis, keepdims=True)
    v = jnp.var(x, axis=axis, keepdims=True)
    return (x - m) / jnp.sqrt(v + eps)

def _scatter_add(tgt, idx, src, axis=0):
    return tgt.at[idx].add(src)

def _segment_sum(src, seg, n):
    return jax.ops.segment_sum(src, seg, n)
kernel_name = 'mk_recurrent_d2_jaxref_r8_4bae57'

def setup_inputs(seed: int=0):
    np.random.seed(seed)
    _w = jnp.asarray

    def _L0_attn_setup():
        import jax, jax.numpy as jnp
        import numpy as np
        HEADS = 16
        DIM_HEAD = 64
        key = jax.random.key(seed)
        ks = jax.random.split(key, 5)
        b, n, dim = (4, 256, 128)
        return {'x': jax.random.normal(ks[0], (b, n, dim), dtype=jnp.float32), 'Wq': jax.random.normal(ks[1], (dim, HEADS * DIM_HEAD), dtype=jnp.float32) * dim ** (-0.5), 'Wkv': jax.random.normal(ks[2], (dim, DIM_HEAD), dtype=jnp.float32) * dim ** (-0.5), 'null_kv': jax.random.normal(ks[3], (DIM_HEAD,), dtype=jnp.float32), 'Wout': jax.random.normal(ks[4], (HEADS * DIM_HEAD, dim), dtype=jnp.float32) * (HEADS * DIM_HEAD) ** (-0.5)}
    _L0_attn_in = _L0_attn_setup()

    def _L0_ffn_setup():
        import jax, jax.numpy as jnp
        import numpy as np
        DIM = 128
        HIDDEN = 384
        SCALE = 1.0 / 127.0

        def _dequant(w_int, dtype):
            return w_int.astype(dtype) * jnp.asarray(SCALE, dtype)
        key = jax.random.key(seed)
        k_x, k_g, k_u, k_d = jax.random.split(key, 4)
        x = jax.random.normal(k_x, (4, 256, DIM), dtype=jnp.float32)
        w_gate = jax.random.randint(k_g, (HIDDEN, DIM), -127, 128, dtype=jnp.int32)
        w_up = jax.random.randint(k_u, (HIDDEN, DIM), -127, 128, dtype=jnp.int32)
        w_down = jax.random.randint(k_d, (DIM, HIDDEN), -127, 128, dtype=jnp.int32)
        return {'x': x, 'w_gate': w_gate, 'w_up': w_up, 'w_down': w_down}
    _L0_ffn_in = _L0_ffn_setup()

    def _L1_attn_setup():
        import jax, jax.numpy as jnp
        import numpy as np
        D_MODEL = 128
        N_HEADS = 16
        HEAD_DIM = D_MODEL // N_HEADS
        key = jax.random.key(seed)
        ks = jax.random.split(key, 5)
        B, T = (4, 256)
        x = jax.random.normal(ks[0], (B, T, D_MODEL), dtype=jnp.float32)
        s_in = 1.0 / np.sqrt(D_MODEL)
        W_qkv = jax.random.normal(ks[1], (D_MODEL, 3 * D_MODEL), dtype=jnp.float32) * s_in
        b_qkv = jnp.zeros((3 * D_MODEL,), dtype=jnp.float32)
        W_proj = jax.random.normal(ks[2], (D_MODEL, D_MODEL), dtype=jnp.float32) * s_in
        b_proj = jnp.zeros((D_MODEL,), dtype=jnp.float32)
        return {'x': x, 'W_qkv': W_qkv, 'b_qkv': b_qkv, 'W_proj': W_proj, 'b_proj': b_proj}
    _L1_attn_in = _L1_attn_setup()

    def _L1_ffn_setup():
        import jax, jax.numpy as jnp
        import numpy as np
        D_MODEL = 128
        M = 64
        INNER = 16
        key = jax.random.key(seed)
        ks = jax.random.split(key, 9)

        def init(k, shape, fan_in):
            bound = 1.0 / np.sqrt(fan_in)
            return jax.random.uniform(k, shape, jnp.float32, -bound, bound)
        x = jax.random.normal(ks[0], (16, 512, D_MODEL), dtype=jnp.float32)
        Win = init(ks[1], (D_MODEL, M), D_MODEL)
        bin_ = init(ks[2], (M,), D_MODEL)
        W1 = init(ks[3], (M, INNER), 1)
        b1 = init(ks[4], (M, INNER), 1)
        W2 = init(ks[5], (M, INNER), INNER)
        b2 = init(ks[6], (M,), INNER)
        Wout = init(ks[7], (M, D_MODEL), M)
        bout = init(ks[8], (D_MODEL,), M)
        return {'x': x, 'Win': Win, 'bin_': bin_, 'W1': W1, 'b1': b1, 'W2': W2, 'b2': b2, 'Wout': Wout, 'bout': bout}
    _L1_ffn_in = _L1_ffn_setup()
    _d = {'L0_attn_x': _L0_attn_in['x'], 'L0_attn_Wq': _L0_attn_in['Wq'], 'L0_attn_Wkv': _L0_attn_in['Wkv'], 'L0_attn_null_kv': _L0_attn_in['null_kv'], 'L0_attn_Wout': _L0_attn_in['Wout'], 'L0_ffn_w_gate': _L0_ffn_in['w_gate'], 'L0_ffn_w_up': _L0_ffn_in['w_up'], 'L0_ffn_w_down': _L0_ffn_in['w_down'], 'L1_attn_W_qkv': _L1_attn_in['W_qkv'], 'L1_attn_b_qkv': _L1_attn_in['b_qkv'], 'L1_attn_W_proj': _L1_attn_in['W_proj'], 'L1_attn_b_proj': _L1_attn_in['b_proj'], 'L1_ffn_Win': _L1_ffn_in['Win'], 'L1_ffn_bin_': _L1_ffn_in['bin_'], 'L1_ffn_W1': _L1_ffn_in['W1'], 'L1_ffn_b1': _L1_ffn_in['b1'], 'L1_ffn_W2': _L1_ffn_in['W2'], 'L1_ffn_b2': _L1_ffn_in['b2'], 'L1_ffn_Wout': _L1_ffn_in['Wout'], 'L1_ffn_bout': _L1_ffn_in['bout']}
    _x0 = _d['L0_attn_x']
    _d['L0_attn_x'] = jax.random.normal(jax.random.fold_in(jax.random.key(seed), 1), (16, 512, 128), dtype=_x0.dtype)
    del _x0
    return _d

def reference(L0_attn_x, L0_attn_Wq, L0_attn_Wkv, L0_attn_null_kv, L0_attn_Wout, L0_ffn_w_gate, L0_ffn_w_up, L0_ffn_w_down, L1_attn_W_qkv, L1_attn_b_qkv, L1_attn_W_proj, L1_attn_b_proj, L1_ffn_Win, L1_ffn_bin_, L1_ffn_W1, L1_ffn_b1, L1_ffn_W2, L1_ffn_b2, L1_ffn_Wout, L1_ffn_bout):

    def _L0_attn_ref(x, Wq, Wkv, null_kv, Wout):
        import jax, jax.numpy as jnp
        import numpy as np
        HEADS = 16
        DIM_HEAD = 64
        b, n, dim = x.shape
        scale = DIM_HEAD ** (-0.5)
        q = (x @ Wq).reshape(b, n, HEADS, DIM_HEAD).transpose(0, 2, 1, 3) * scale
        kv = x @ Wkv
        kv = jnp.concatenate([jnp.broadcast_to(null_kv, (b, 1, DIM_HEAD)), kv], axis=1)
        sim = jnp.einsum('bhid,bjd->bhij', q, kv)
        mask_value = -jnp.finfo(sim.dtype).max
        i, j = (sim.shape[-2], sim.shape[-1])
        causal_mask = jnp.triu(jnp.ones((i, j), dtype=bool), k=j - i + 1)
        sim = jnp.where(causal_mask, mask_value, sim)
        attn = jax.nn.softmax(sim.astype(jnp.float32), axis=-1)
        out = jnp.einsum('bhij,bjd->bhid', attn, kv.astype(jnp.float32))
        out = out.transpose(0, 2, 1, 3).reshape(b, n, HEADS * DIM_HEAD)
        return out @ Wout

    def _L0_ffn_ref(x, w_gate, w_up, w_down):
        import jax, jax.numpy as jnp
        import numpy as np
        DIM = 128
        HIDDEN = 384
        SCALE = 1.0 / 127.0

        def _dequant(w_int, dtype):
            return w_int.astype(dtype) * jnp.asarray(SCALE, dtype)
        wg = _dequant(w_gate, x.dtype)
        wu = _dequant(w_up, x.dtype)
        wd = _dequant(w_down, x.dtype)
        gate = jnp.einsum('bsd,hd->bsh', x, wg)
        up = jnp.einsum('bsd,hd->bsh', x, wu)
        h = jax.nn.silu(gate) * up
        return jnp.einsum('bsh,dh->bsd', h, wd)

    def _L1_attn_ref(x, W_qkv, b_qkv, W_proj, b_proj):
        import jax, jax.numpy as jnp
        import numpy as np
        D_MODEL = 128
        N_HEADS = 16
        HEAD_DIM = D_MODEL // N_HEADS
        B, T, C = x.shape
        qkv = x @ W_qkv + b_qkv
        q, k, v = jnp.split(qkv, 3, axis=-1)

        def heads(t):
            return t.reshape(B, T, N_HEADS, HEAD_DIM).transpose(0, 2, 1, 3)
        q, k, v = (heads(q), heads(k), heads(v))
        scale = 1.0 / np.sqrt(HEAD_DIM)
        att = jnp.einsum('bhqd,bhkd->bhqk', q, k) * scale
        causal = jnp.tril(jnp.ones((T, T), dtype=bool))
        att = jnp.where(causal, att, -jnp.inf)
        att = jax.nn.softmax(att, axis=-1)
        out = jnp.einsum('bhqk,bhkd->bhqd', att, v)
        out = out.transpose(0, 2, 1, 3).reshape(B, T, C)
        return out @ W_proj + b_proj

    def _L1_ffn_ref(x, Win, bin_, W1, b1, W2, b2, Wout, bout):
        import jax, jax.numpy as jnp
        import numpy as np
        D_MODEL = 128
        M = 64
        INNER = 16
        s = jnp.einsum('btd,dm->btm', x, Win) + bin_
        h = jax.nn.relu(s[..., None] * W1 + b1)
        g = jnp.einsum('btmh,mh->btm', h, W2) + b2
        out = jnp.einsum('btm,md->btd', g, Wout) + bout
        return out
    x = L0_attn_x
    xn = _layernorm(x, axis=-1)
    s = _L0_attn_ref(xn, L0_attn_Wq, L0_attn_Wkv, L0_attn_null_kv, L0_attn_Wout)
    g = _silu(_L0_ffn_ref(xn, L0_ffn_w_gate, L0_ffn_w_up, L0_ffn_w_down))
    x = x + s * g
    xn = _layernorm(x, axis=-1)
    s = _L1_attn_ref(xn, L1_attn_W_qkv, L1_attn_b_qkv, L1_attn_W_proj, L1_attn_b_proj)
    g = _silu(_L1_ffn_ref(xn, L1_ffn_Win, L1_ffn_bin_, L1_ffn_W1, L1_ffn_b1, L1_ffn_W2, L1_ffn_b2, L1_ffn_Wout, L1_ffn_bout))
    x = x + s * g
    return x

_drawn_inputs = setup_inputs


def setup_inputs(seed=0):
    import zlib

    import numpy as np

    out = dict(_drawn_inputs(seed))
    spreads = {'L1_attn_b_qkv': (0.0, 0.8), 'L1_attn_b_proj': (0.0, 2.0)}
    factors = {'L1_attn_W_qkv': 8.0,
     'L1_attn_W_proj': 8.0,
     'L1_ffn_Win': 8.0,
     'L1_ffn_bin_': 8.0,
     'L1_ffn_W1': 8.0,
     'L1_ffn_b1': 8.0,
     'L1_ffn_W2': 8.0,
     'L1_ffn_b2': 24.301,
     'L1_ffn_Wout': 8.0,
     'L1_ffn_bout': 200.0}
    for name, (base, spread) in spreads.items():
        noise = np.random.default_rng([zlib.crc32(name.encode()), seed]).standard_normal(out[name].shape)
        drawn = base * np.exp(spread * noise) if base else spread * noise
        out[name] = jnp.asarray(drawn.astype(out[name].dtype))
    for name, factor in factors.items():
        out[name] = (out[name] * factor).astype(out[name].dtype)
    return out
```

```python
from contextlib import ExitStack

import numpy as np

import concourse.bass as bass
from concourse import mybir

F32 = mybir.dt.float32
F32R = mybir.dt.float32r
BF16 = mybir.dt.bfloat16
I32 = mybir.dt.int32
ALU = mybir.AluOpType
ACT = mybir.ActivationFunctionType

P = 128
B, T, D = 16, 512, 128
NB = T // P
H = 16
NG = 4
GH = H // NG
D0 = 64
D1 = D // H
HID = 384
NHID = HID // P
M1, IN1 = 64, 16
NE = M1 * IN1 // P
EPS = 1e-5
CHAIN = 25
NEG = -1e30
DEQ = 1.0 / 127.0

RES = {}
_at = 0
for _name, _n in [("ident", P), ("wkv", P), ("vs", P), ("maskq", T), ("maskk", P), ("onehot", NG * 32), ("lowmask", 3),
                  ("bqk", 2 * NG), ("bqk_low", 2 * NG), ("wv", P), ("bv", P), ("wp", P), ("bp", P), ("win", P),
                  ("bin", 1), ("w1", NE), ("b1", NE), ("w2", NE * 32), ("b2", 1), ("wo1", P), ("bout", P)]:
    RES[_name] = (_at, _at + _n)
    _at += _n
NRES = _at
STG = {"wq": (0, 2048), "qk": (2048, 3072), "sel": (3072, 4096), "exp": (4096, 5120)}
NSTG = 5120
ST2 = {"nullsel": (0, 1024), "null": (1024, 1088)}
NST2 = 1088

KOFF = (0, 512, 1024, 896)


def kw(kb):
    return T - P * kb


def schedule():
    s = [("xt", 0), ("kv",), ("vs",)]
    s += [("prep0", 0), ("prep0", 1), ("sm", 0, 0), ("prep0", 2), ("sm", 0, 1), ("prep0", 3), ("sm", 0, 2), ("sm", 0, 3)]
    s += [("ytop", 0), ("max", 0, 0)]
    s += [("gate", 0), ("up", 0), ("mt", 0, 0), ("gate", 1), ("up", 1), ("gate", 2), ("up", 2), ("down",)]
    for g in range(NG):
        h, more = GH * g, g + 1 < NG
        s += [("st", 0, h)]
        if more:
            s += [("prep0", h + 4), ("prep0", h + 5), ("sm", 0, h + 4)]
        s += [("st", 0, h + 1)]
        if more:
            s += [("sm", 0, h + 5), ("prep0", h + 6)]
        s += [("st", 0, h + 2)]
        if more:
            s += [("sm", 0, h + 6), ("prep0", h + 7)]
        s += [("av0", h // 2), ("st", 0, h + 3)]
        if more:
            s += [("sm", 0, h + 7), ("ytop", g + 1), ("max", 0, g + 1)]
        s += [("av0", h // 2 + 1)]
        if more:
            s += [("mt", 0, g + 1)]
        s += [("den", g)]
    s += [("lt",), ("rt",)] + [("norm", p) for p in range(H // 2)] + [("out0",)]
    s += [("xt", 1), ("prep1", 0), ("sm", 1, 0), ("sm", 1, 1), ("sm", 1, 2), ("sm", 1, 3), ("max", 1, 0)]
    s += [("v1",), ("s1",), ("ex", 0), ("ex", 1), ("mt", 1, 0)] + [("ex", i) for i in range(2, NE)] + [("con",), ("ffo",)]
    for g in range(NG):
        h, more = GH * g, g + 1 < NG
        s += [("st", 1, h)]
        if more:
            s += [("prep1", g + 1)]
        s += [("st", 1, h + 1)]
        if more:
            s += [("sm", 1, h + 4)]
        s += [("st", 1, h + 2)]
        if more:
            s += [("sm", 1, h + 5), ("sm", 1, h + 6)]
        s += [("st", 1, h + 3)]
        if more:
            s += [("sm", 1, h + 7), ("max", 1, g + 1), ("mt", 1, g + 1)]
        s += [("av1", g)]
    s += [("tr", n) for n in range(NB)] + [("att",), ("proj",)]
    return s


def bank_plan(steps):
    uses, order = [0] * 8, {}

    def take(name, bank):
        order[name] = (bank, uses[bank])
        uses[bank] += 1

    n_sm = 0
    for st in steps:
        kind = st[0]
        if kind == "st":
            for u in range(3):
                take(st + (u,), u)
        elif kind == "sm":
            for u in range(3):
                take(st + (u,), 3 + n_sm % 2)
                n_sm += 1
        elif kind == "prep1":
            take(("prep1", "q", st[1]), 7)
            take(("prep1", "k", st[1]), 6)
        elif kind in ("xt", "gate", "down", "av0", "s1", "av1"):
            take(st, 5)
        elif kind in ("kv", "up", "rt", "out0", "v1", "ffo"):
            take(st, 6)
        elif kind in ("vs", "prep0", "mt", "lt", "proj"):
            take(st, 7)
        elif kind == "norm":
            take(st, 5 + 2 * (st[1] % 2))
        elif kind == "ex":
            take(st, 6 + st[1] % 2)
        elif kind == "con":
            take(st, 5)
        elif kind == "den":
            if st[1] == 0:
                take(("den",), 6)
        elif kind == "tr":
            take(st, 5 + st[1] % 2)
        elif kind == "att":
            take(st, 6)
    return order, uses


def two_layers(nc, x_d, res_d, stg_d, st2_d, wout_d, wg_d, wu_d, wd_d, out_d):
    steps = schedule()
    unit, uses = bank_plan(steps)
    with ExitStack() as ctx:
        def sb(name, shape, dt=F32):
            return ctx.enter_context(nc.sbuf_tensor(name, shape, dt))

        def sem(name):
            return ctx.enter_context(nc.semaphore(name))

        res = sb("res", [P, NRES])
        wq_lead, wq_rest = sb("wq_lead", [P, H, P], F32R), sb("wq_rest", [P, H, P], F32R)
        wgu_lead, wgu_rest = sb("wgu_lead", [P, 2, NHID, P], F32R), sb("wgu_rest", [P, 2, NHID, P], F32R)
        qk_lead, qk_rest = sb("qk_lead", [P, 2, NG, P], F32R), sb("qk_rest", [P, 2, NG, P], F32R)
        sel = sb("sel", [P, H // 2, P], F32R)
        spread = sb("spread", [P, NE, P], F32R)
        wout = sb("wout", [P, H // 2, P])
        wdown = sb("wdown", [P, NHID, P])
        null_out = sb("null_out", [P, P])
        ident_b, maskk_b = sb("ident_b", [P, P], BF16), sb("maskk_b", [P, P], BF16)
        half_neg = sb("half_neg", [P, NB])

        x_t, x1_t, xn, out_t = sb("x_t", [P, NB, D]), sb("x1_t", [P, NB, D]), sb("xn", [P, NB, D]), sb("out_t", [P, NB, D])
        stats, mv, var_e, rstd = sb("stats", [P, NB, 6]), sb("mv", [P, NB, 2]), sb("var_e", [P, NB]), sb("rstd", [P, NB])
        xf, x_lead, x_rest = sb("xf", [P, T]), sb("x_lead", [P, T], F32R), sb("x_rest", [P, T], F32R)
        k_lead, k_rest = sb("k_lead", [P, T], F32R), sb("k_rest", [P, T], F32R)
        v0, s_null = sb("v0", [P, NB, D0]), sb("s_null", [P, H, NB])
        cut = sb("cut", [P, 2, T], F32R)
        q_two = sb("q_two", [P, 2 * GH, T], F32R)
        q_max = sb("q_max", [P, 2 * GH, T], F32R)
        o0 = sb("o0", [P, H // 2, T])
        probs = sb("probs", [P, GH, 1280])
        q1_st, q1_max, k1_st = q_two[:, 0:2], q_two[:, 2:4], q_two[:, 4:6]
        k1_head = sb("k1_head", [P, 2 * GH, T], F32R)
        v1 = sb("v1", [P, NB, H, 32])
        rowmax, max_parts = sb("rowmax", [P, GH, NB]), sb("max_parts", [P, 2, 2 * GH * NB])
        max_t = sb("max_t", [2 * GH * NB, 2, P], F32R)
        p_arg, p_null = sb("p_arg", [P, H, NB]), sb("p_null", [P, H, NB])
        den_s = sb("den_s", [P, T])
        den_t, rec = sb("den_t", [P, H, NB]), sb("rec", [P, H, NB])
        rt_in = sb("rt_in", [P, NB, P])
        rt_r, rt_f = sb("rt_r", [P, T], F32R), sb("rt_f", [P, T])
        o1 = sb("o1", [P, NG, T])
        th, hg, hidden = sb("th", [P, T]), sb("hg", [P, T]), o1[:, 0:NHID]
        gated, ffn_th = sb("gated", [P, T]), th
        s_parts = sb("s_parts", [P, T], F32R)
        pieces = o0
        g1, f1 = rt_f, hg
        rec1, att, att_t = sb("rec1", [P, 2, H]), sb("att", [P, NB, H, D1]), den_s
        masked = sb("masked", [P, 2, T])
        banks = [ctx.enter_context(nc.psum_tensor(f"bank{n}", [P, T], F32)) for n in range(8)]
        stage = probs[:].rearrange("p h c -> p (h c)")
        stage2 = o0[:].rearrange("p h c -> p (h c)")
        stage_i = o1[:].rearrange("p h c -> p (h c)").bitcast(I32)

        def R(name):
            return res[:, RES[name][0]:RES[name][1]]

        ident = R("ident")

        counts = {}

        def counting(name, per, step=1, base=0):
            s = sem(name)
            counts[s.name] = per, step, base
            return s

        def count(i, s, n):
            per, step, base = counts[s.name]
            return i * (per * step) + (n + base) * step

        bank_filled = [sem(f"bank{n}_filled") for n in range(8)]
        bank_drained = [sem(f"bank{n}_drained") for n in range(8)]
        x_loaded, out_stored = counting("x_loaded", 1, 16), counting("out_stored", 1, 16, 1)
        var_made, rstd_made, xn_made = counting("var_made", 2), counting("rstd_made", 2), counting("xn_made", 2)
        x1_made, out_made = counting("x1_made", 1), counting("out_made", 1)
        lead_made = counting("lead_made", sum({"xt": 1, "kv": 1, "prep0": 1, "s1": 1, "prep1": 2}.get(s[0], 0) for s in steps))
        parts_made = counting("parts_made", 2 * NG)
        y_top, y_rows = counting("y_top", NG, 16), counting("y_rows", NG, 16)
        q1_copied, q1_rows = counting("q1_copied", NG, 16), counting("q1_rows", NG * GH, 16)
        k1_spread = counting("k1_spread", H, 16)
        p_arg_made, p_null_made = counting("p_arg_made", NG), counting("p_null_made", NG)
        probs_used, rt_made = counting("probs_used", NG - 1), counting("rt_made", 1)
        th_made = counting("th_made", NHID + 2)
        dve_chain = counting("dve_chain", CHAIN)
        passed = sem("passed")
        loads, setup_v, setup_p, setup_g, setup_b = sem("loads"), sem("setup_v"), sem("setup_p"), sem("setup_g"), sem("setup_b")

        def plan(name):
            return unit[name[0] if isinstance(name[0], tuple) else name]

        def bank(*name):
            return banks[plan(name)[0]]

        def filled(*name):
            return bank_filled[plan(name)[0]]

        def drained(*name):
            return bank_drained[plan(name)[0]]

        def nth(i, *name):
            b, k = plan(name)
            return i * uses[b] + (k + 1)

        def after(i, *name):
            b, k = plan(name)
            return i * uses[b] + (k + 2)

        lead_of, n = {}, 0
        for stp in steps:
            if stp[0] in ("xt", "kv", "prep0", "s1"):
                n += 1
                lead_of[stp] = n
            if stp[0] == "prep1":
                n += 2
                lead_of[stp] = n
        cut_at = {}
        for stp in steps:
            if stp[0] == "prep0":
                cut_at[stp] = len(cut_at) % 2

        block = ctx.enter_context(nc.Block())

        @block.sync
        def _(sp):
            sp.dma_start(res[:], res_d).then_inc(loads, 16)
            sp.dma_start(stage[:, 0:NSTG], stg_d).then_inc(loads, 16)
            sp.dma_start(stage2[:, 0:NST2], st2_d).then_inc(loads, 16)
            sp.dma_start(wout[:], wout_d.rearrange("(c p) n -> p c n", p=P)).then_inc(loads, 16)
            sp.dma_start(stage_i[:, 0:HID], wg_d).then_inc(loads, 16)
            sp.dma_start(stage_i[:, HID:2 * HID], wu_d).then_inc(loads, 16)
            sp.dma_start(stage_i[:, 2 * HID:3 * HID].rearrange("p (c n) -> p c n", c=NHID),
                         wd_d.rearrange("(c p) n -> p c n", p=P)).then_inc(loads, 16)
            xv = x_d.rearrange("b (n p) d -> b p n d", p=P)
            ov = out_d.rearrange("b (n p) d -> b p n d", p=P)
            sp.dma_start(x_t[:], xv[0]).then_inc(x_loaded, 16)
            with sp.Fori(0, B) as i:
                for stp in steps:
                    kind = stp[0]
                    if kind == "ytop":
                        g = stp[1]
                        s0 = GH * (g % 2)
                        sp.wait_ge(drained("prep0", GH * g + 3), after(i, "prep0", GH * g + 3))
                        sp.sem_inc(passed, 1)
                        if g >= 2:
                            sp.wait_ge(drained("st", 0, GH * (g - 2) + 3, 2), after(i, "st", 0, GH * (g - 2) + 3, 2))
                            sp.sem_inc(passed, 1)
                        sp.dma_start(q_max[0:D0, s0:s0 + GH, :].bitcast(F32), q_two[0:D0, s0:s0 + GH, :].bitcast(F32)).then_inc(y_top, 16)
                    elif kind == "mt":
                        layer, g = stp[1:]
                        src = max_t[:, g % 2, :].bitcast(F32)
                        sp.wait_ge(drained(stp), after(i, stp))
                        sp.sem_inc(passed, 1)
                        if layer == 0:
                            s0 = GH * (g % 2)
                            sp.dma_start(q_max[D0:D0 + 2, s0:s0 + GH, :].bitcast(F32), src).then_inc(y_rows, 16)
                        else:
                            sp.wait_ge(q1_copied, count(i, q1_copied, g + 1))
                            sp.sem_inc(passed, 1)
                            for j in range(GH):
                                sp.dma_start(q1_max[32 * j + 24:32 * j + 26, g % 2, :].bitcast(F32),
                                                          src[8 * j:8 * j + 8]).then_inc(q1_rows, 16)
                    elif kind == "prep1":
                        g = stp[1]
                        sp.wait_ge(drained("prep1", "q", g), after(i, "prep1", "q", g))
                        sp.sem_inc(passed, 1)
                        if g >= 2:
                            sp.wait_ge(drained("st", 1, GH * (g - 2) + 3, 2), after(i, "st", 1, GH * (g - 2) + 3, 2))
                            sp.sem_inc(passed, 1)
                        sp.dma_start(q1_max[:, g % 2, :].bitcast(F32), q1_st[:, g % 2, :].bitcast(F32)).then_inc(q1_copied, 16)
                        sp.wait_ge(drained("prep1", "k", g), after(i, "prep1", "k", g))
                        sp.sem_inc(passed, 1)
                        for j in range(GH):
                            sp.dma_start(k1_head[32 * j:32 * j + 32, GH * (g % 2) + j, :].bitcast(F32),
                                                        k1_st[32 * j:32 * j + 32, g % 2, :].bitcast(F32)).then_inc(k1_spread, 16)
                    elif kind == "out0":
                        sp.wait_ge(x1_made, count(i, x1_made, 1))
                        sp.sem_inc(passed, 1)
                        sp.dma_start(x_t[:], xv[(i + 1) % B]).then_inc(x_loaded, 16)
                sp.wait_ge(out_made, count(i, out_made, 1))
                sp.sem_inc(passed, 1)
                sp.dma_start(ov[i], out_t[:]).then_inc(out_stored, 16)
            sp.wait_ge(out_stored, 16 * (B + 1))
            sp.wait_ge(x_loaded, 16 * (B + 1))

        @block.gpsimd
        def _(pool):
            for b in range(8):
                pool.sem_inc(bank_drained[b], 1)
            pool.sem_inc(out_stored, 16)
            nc.gpsimd.memset(half_neg[:], -0.5).then_inc(setup_g, 1)
            nc.gpsimd.memset(q_max[:].bitcast(F32), 0.0).then_inc(setup_g, 1)
            nc.gpsimd.memset(k1_head[:].bitcast(F32), 0.0).then_inc(setup_g, 1)
            nc.gpsimd.memset(k_rest[:].bitcast(F32), 0.0).then_inc(setup_g, 1)
            nc.gpsimd.memset(rt_in[:], 0.0).then_inc(setup_g, 1)
            nc.gpsimd.memset(v1[:], 0.0).then_inc(setup_g, 1)
            pool.wait_ge(setup_g, 6)
            nc.gpsimd.memset(k_rest[D0:D0 + 2, :].bitcast(F32), -1.0).then_inc(setup_g, 1)
            pool.wait_ge(setup_g, 7)
            nc.gpsimd.memset(v1[:, :, :, D1], 1.0).then_inc(setup_g, 1)
            pool.wait_ge(setup_g, 8)
            with pool.Fori(0, B) as i:
                for layer in range(2):
                    pool.wait_ge(var_made, count(i, var_made, layer + 1))
                    nc.gpsimd.tensor_tensor(rstd[:], var_e[:], half_neg[:], ALU.pow).then_inc(rstd_made, 1)

        @block.scalar
        def _(act):
            def copy(out, in_):
                return nc.scalar.activation(out, in_, ACT.Copy)

            act.wait_ge(loads, 16 * 7)
            act.wait_ge(setup_v, 1)
            act.wait_ge(setup_g, 8)
            with act.Fori(0, B) as i:
                for stp in steps:
                    kind = stp[0]
                    if kind == "xt":
                        act.wait_ge(filled(stp), nth(i, stp))
                        ps = bank(stp)
                        copy(xf[:], ps[:])
                        copy(x_lead[:], ps[:]).then_inc(lead_made, 1)
                    elif kind == "kv":
                        act.wait_ge(filled(stp), nth(i, stp))
                        ps = bank(stp)
                        copy(k_lead[:], ps[:]).then_inc(lead_made, 1)
                    elif kind == "prep0":
                        act.wait_ge(filled(stp), nth(i, stp))
                        ps = bank(stp)
                        h = stp[1]
                        if h >= 2:
                            act.wait_ge(drained("prep0", h - 2), after(i, "prep0", h - 2))
                        nc.scalar.activation(cut[:, cut_at[stp], :], ps[:], ACT.Copy, scale=R("lowmask")[:, 0:1]).then_inc(lead_made, 1)
                    elif kind == "prep1":
                        g = stp[1]
                        for n, which in enumerate("qk"):
                            act.wait_ge(filled("prep1", which, g), nth(i, "prep1", which, g))
                            ps = bank("prep1", which, g)
                            if g >= 1:
                                act.wait_ge(drained("prep1", which, g - 1), after(i, "prep1", which, g - 1))
                            nc.scalar.activation(cut[:, n, :], ps[:], ACT.Identity,
                                                                scale=R("lowmask")[:, 1 + n:2 + n],
                                                                bias=R("bqk_low")[:, NG * n + g:NG * n + g + 1]).then_inc(lead_made, 1)
                    elif kind == "mt":
                        layer, g = stp[1:]
                        act.wait_ge(filled(stp), nth(i, stp))
                        ps = bank(stp)
                        copy(max_t[:, g % 2, :], ps[0:2 * GH * NB, 0:P]).then_inc(drained(stp), 1)
                        if layer == 0:
                            act.wait_ge(p_arg_made, count(i, p_arg_made, g + 1))
                            nc.scalar.activation(p_null[:, GH * g:GH * g + GH, :], p_arg[:, GH * g:GH * g + GH, :],
                                                                  ACT.Exp, scale=D0 ** -0.5).then_inc(p_null_made, 1)
                    elif kind == "st":
                        layer, h = stp[1:]
                        scale = float(D0 if layer == 0 else D1) ** -0.5
                        if layer == 0 and h >= GH:
                            act.wait_ge(probs_used, count(i, probs_used, h // GH))
                        pr = probs[:, h % GH, :]
                        for u, (a, b) in enumerate(((0, 512), (512, 1024), (1024, 1280))):
                            act.wait_ge(filled(stp + (u,)), nth(i, stp + (u,)))
                            ps = bank(stp + (u,))
                            nc.scalar.activation(pr[:, a:b], ps[:, 0:b - a], ACT.Exp, scale=scale).then_inc(drained(stp + (u,)), 1)
                    elif kind == "gate":
                        act.wait_ge(filled(stp), nth(i, stp))
                        ps = bank(stp)
                        if stp[1] >= 1:
                            act.wait_ge(drained("gate", stp[1] - 1), after(i, "gate", stp[1] - 1))
                        nc.scalar.activation(th[:], ps[:], ACT.Tanh, scale=0.5).then_inc(th_made, 1)
                    elif kind == "down":
                        act.wait_ge(filled(stp), nth(i, stp))
                        ps = bank(stp)
                        nc.scalar.activation(ffn_th[:], ps[:], ACT.Tanh, scale=0.5).then_inc(th_made, 1)
                    elif kind == "av0":
                        act.wait_ge(filled(stp), nth(i, stp))
                        ps = bank(stp)
                        copy(o0[:, stp[1], :], ps[:]).then_inc(drained(stp), 1)
                    elif kind == "lt":
                        act.wait_ge(filled("den"), nth(i, "den"))
                        ps = bank("den")
                        copy(den_s[:], ps[:]).then_inc(drained("den"), 1)
                    elif kind == "rt":
                        act.wait_ge(filled(stp), nth(i, stp))
                        ps = bank(stp)
                        copy(rt_r[:], ps[:])
                        copy(rt_f[:], ps[:]).then_inc(drained(stp), 1)
                    elif kind == "s1":
                        act.wait_ge(filled(stp), nth(i, stp))
                        ps = bank(stp)
                        nc.scalar.activation(s_parts[:], ps[:], ACT.Identity, bias=R("bin")).then_inc(lead_made, 1)
                    elif kind == "ex":
                        n = stp[1]
                        act.wait_ge(filled(stp), nth(i, stp))
                        ps = bank(stp)
                        nc.scalar.activation(pieces[:, n, :], ps[:], ACT.Relu, scale=R("w1")[:, n:n + 1],
                                                   bias=R("b1")[:, n:n + 1]).then_inc(drained(stp), 1)
                    elif kind == "con":
                        act.wait_ge(filled(stp), nth(i, stp))
                        ps = bank(stp)
                        nc.scalar.activation(g1[:], ps[:], ACT.Identity, bias=R("b2")).then_inc(drained(stp), 1)
                    elif kind == "ffo":
                        act.wait_ge(drained(stp), after(i, stp))
                        nc.scalar.activation(ffn_th[:], f1[:], ACT.Tanh, scale=0.5).then_inc(th_made, 1)
                    elif kind == "av1":
                        act.wait_ge(filled(stp), nth(i, stp))
                        ps = bank(stp)
                        copy(o1[:, stp[1], :], ps[:]).then_inc(drained(stp), 1)
                    elif kind == "att":
                        act.wait_ge(filled(stp), nth(i, stp))
                        ps = bank(stp)
                        copy(att_t[:], ps[:]).then_inc(drained(stp), 1)

        @block.vector
        def _(dve):
            v = nc.vector

            dve.wait_ge(loads, 16 * 7)
            n = 0

            def setup(ins):
                nonlocal n
                n += 1
                ins.then_inc(setup_b, 1)
                dve.wait_ge(setup_b, n)

            def stg(name):
                return stage[:, STG[name][0]:STG[name][1]]

            def cut_weights(lead, rest, full):
                setup(v.tensor_copy(lead, full))
                setup(v.tensor_tensor(rest, full, lead.bitcast(F32), ALU.subtract))

            cut_weights(wq_lead[:].rearrange("p h n -> p (h n)"), wq_rest[:].rearrange("p h n -> p (h n)"), stg("wq"))
            cut_weights(qk_lead[:].rearrange("p a g n -> p (a g n)"), qk_rest[:].rearrange("p a g n -> p (a g n)"), stg("qk"))
            setup(v.tensor_copy(sel[:].rearrange("p h n -> p (h n)"), stg("sel")))
            setup(v.tensor_copy(spread[:].rearrange("p h n -> p (h n)"), stg("exp")))
            setup(v.tensor_copy(ident_b[:], ident))
            setup(v.tensor_copy(maskk_b[:], R("maskk")))
            null_row = stage2[:, ST2["null"][0]:ST2["null"][1]]
            for h in range(H):
                setup(v.tensor_tensor(masked[:, 0, 0:D0], stg("wq")[:, P * h:P * h + D0], null_row, ALU.mult))
                setup(v.tensor_reduce(R("vs")[:, D0 + h:D0 + h + 1], masked[:, 0, 0:D0], mybir.AxisListType.X, ALU.add))
            deq = stage[:, 0:3 * HID]
            setup(v.tensor_copy(deq, stage_i[:, 0:3 * HID]))
            setup(v.tensor_scalar(deq, deq, DEQ, None, ALU.mult))
            cut_weights(wgu_lead[:].rearrange("p a c n -> p (a c n)"), wgu_rest[:].rearrange("p a c n -> p (a c n)"), deq[:, 0:2 * HID])
            setup(v.tensor_scalar(wdown[:].rearrange("p c n -> p (c n)"), deq[:, 2 * HID:3 * HID], 0.5, None, ALU.mult))
            dve.wait_ge(setup_p, 1)
            setup(v.tensor_copy(null_out[:], banks[0][:, 0:P]))
            v.tensor_copy(masked[:, 0, 0:1], ident[:, 0:1]).then_inc(setup_v, 1)

            with dve.Fori(0, B) as i:
                chained = iter(range(1, CHAIN + 1))

                def layer_norm(src, layer):
                    for n in range(NB):
                        last = v.bn_stats(stats[:, n, :], src[:, n, :])
                    last.then_inc(dve_chain, 1)
                    dve.wait_ge(dve_chain, count(i, dve_chain, next(chained)))
                    dve.sem_inc(passed, 1)
                    for n in range(NB):
                        last = v.bn_aggr(mv[:, n, :], stats[:, n, :])
                    last.then_inc(dve_chain, 1)
                    dve.wait_ge(dve_chain, count(i, dve_chain, next(chained)))
                    v.tensor_scalar(var_e[:], mv[:, :, 1], EPS, None, ALU.add).then_inc(var_made, 1)
                    dve.wait_ge(rstd_made, count(i, rstd_made, layer + 1))
                    for n in range(NB):
                        last = v.tensor_scalar(xn[:, n, :], src[:, n, :], mv[:, n, 0:1], rstd[:, n:n + 1], ALU.subtract, ALU.mult)
                    last.then_inc(xn_made, 1)

                for stp in steps:
                    kind = stp[0]
                    if kind == "xt":
                        if stp[1] == 0:
                            dve.wait_ge(x_loaded, count(i, x_loaded, 1))
                        layer_norm(x_t if stp[1] == 0 else x1_t, stp[1])
                        dve.wait_ge(lead_made, count(i, lead_made, lead_of[stp]))
                        ps = bank(stp)
                        v.tensor_tensor(x_rest[:], ps[:], x_lead[:].bitcast(F32), ALU.subtract).then_inc(drained(stp), 1)
                    elif kind == "kv":
                        dve.wait_ge(lead_made, count(i, lead_made, lead_of[stp]))
                        ps = bank(stp)
                        v.tensor_tensor(k_rest[0:D0, :], ps[0:D0, :], k_lead[0:D0, :].bitcast(F32), ALU.subtract).then_inc(drained(stp), 1)
                    elif kind == "vs":
                        dve.wait_ge(filled(stp), nth(i, stp))
                        ps = bank(stp)[:].rearrange("p (n c) -> p n c", n=NB)
                        v.tensor_copy(v0[:], ps[:, :, 0:D0])
                        v.tensor_copy(s_null[:].rearrange("p h n -> p n h"), ps[:, :, D0:D0 + H]).then_inc(drained(stp), 1)
                    elif kind == "prep0":
                        h = stp[1]
                        dve.wait_ge(lead_made, count(i, lead_made, lead_of[stp]))
                        ps = bank(stp)
                        if h >= 2 * GH:
                            dve.wait_ge(drained("st", 0, h - 2 * GH, 2), after(i, "st", 0, h - 2 * GH, 2))
                            dve.wait_ge(y_top, count(i, y_top, h // GH - 1))
                        v.tensor_tensor(q_two[:, h % (2 * GH), :], ps[:], cut[:, cut_at[stp], :].bitcast(F32), ALU.subtract).then_inc(drained(stp), 1)
                    elif kind == "prep1":
                        g = stp[1]
                        for n, (which, dst) in enumerate((("q", q1_st), ("k", k1_st))):
                            dve.wait_ge(lead_made, count(i, lead_made, lead_of[stp] - 1 + n))
                            ps = bank("prep1", which, g)
                            if g >= 2 and n == 0:
                                dve.wait_ge(q1_copied, count(i, q1_copied, g - 1))
                                dve.wait_ge(drained("st", 1, GH * (g - 2) + 3, 2), after(i, "st", 1, GH * (g - 2) + 3, 2))
                            if g >= 2 and n == 1:
                                dve.wait_ge(k1_spread, count(i, k1_spread, GH * (g - 1)))
                            v.scalar_tensor_tensor(dst[:, g % 2, :], ps[:], R("bqk")[:, NG * n + g:NG * n + g + 1],
                                                         cut[:, n, :].bitcast(F32), ALU.add, ALU.subtract).then_inc(drained("prep1", which, g), 1)
                    elif kind == "sm":
                        layer, h = stp[1:]
                        for u, blocks in enumerate(((3,), (2, 0), (1,))):
                            dve.wait_ge(filled(stp + (u,)), nth(i, stp + (u,)))
                            ps = bank(stp + (u,))
                            out = masked[:, unit[stp + (u,)][0] - 3]
                            dve.sem_inc(passed, 1)
                            for qb in blocks:
                                w, at = P * (qb + 1), (384 if qb == 0 else 0)
                                last = v.tensor_tensor_reduce(out[:, at:at + w], ps[:, at:at + w], R("maskq")[:, T - w:T], 1.0, -3e38,
                                                              ALU.add, ALU.max, rowmax[:, h % GH, qb:qb + 1])
                            last.then_inc(drained(stp + (u,)), 1)
                    elif kind == "max":
                        layer, g = stp[1:]
                        n = 16
                        dve.wait_ge(drained("sm", layer, GH * g + 3, 2), after(i, "sm", layer, GH * g + 3, 2))
                        if layer == 0:
                            sn = s_null[:, GH * g:GH * g + GH, :]
                            v.tensor_tensor(rowmax[:], rowmax[:], sn, ALU.max).then_inc(dve_chain, 1)
                            dve.wait_ge(dve_chain, count(i, dve_chain, next(chained)))
                            mp = max_parts[:, g % 2, :].rearrange("p (c h n) -> p c h n", c=2, h=GH)
                            lead, rest = mp[:, 0], mp[:, 1]
                        else:
                            mp = max_parts[:, g % 2, :].rearrange("p (h c n) -> p h c n", c=2, h=GH)
                            lead, rest = mp[:, :, 0], mp[:, :, 1]
                        if layer == 0:
                            v.tensor_tensor(p_arg[:, GH * g:GH * g + GH, :], sn, rowmax[:], ALU.subtract).then_inc(p_arg_made, 1)
                        v.tensor_copy(lead.bitcast(F32R), rowmax[:]).then_inc(dve_chain, 1)
                        dve.wait_ge(dve_chain, count(i, dve_chain, next(chained)))
                        v.tensor_tensor(rest, rowmax[:], lead, ALU.subtract).then_inc(parts_made, 1)
                    elif kind == "gate":
                        dve.wait_ge(th_made, count(i, th_made, stp[1] + 1))
                        if stp[1] >= 1:
                            dve.wait_ge(drained("up", stp[1] - 1), after(i, "up", stp[1] - 1))
                        ps = bank(stp)
                        v.scalar_tensor_tensor(hg[:], th[:], 1.0, ps[:], ALU.add, ALU.mult).then_inc(drained(stp), 1)
                    elif kind == "up":
                        dve.wait_ge(filled(stp), nth(i, stp))
                        ps = bank(stp)
                        dve.wait_ge(drained("gate", stp[1]), after(i, "gate", stp[1]))
                        v.tensor_tensor(hidden[:, stp[1], :], ps[:], hg[:], ALU.mult).then_inc(drained(stp), 1)
                    elif kind == "down":
                        dve.wait_ge(th_made, count(i, th_made, NHID + 1))
                        ps = bank(stp)
                        v.scalar_tensor_tensor(gated[:], ffn_th[:], 1.0, ps[:], ALU.add, ALU.mult).then_inc(drained(stp), 1)
                    elif kind == "lt":
                        dve.wait_ge(filled(stp), nth(i, stp))
                        ps = bank(stp)
                        d = ps[:].rearrange("p (n j c) -> p n j c", n=NB, j=GH)
                        for g in range(NG):
                            if g == NG - 1:
                                dve.wait_ge(p_null_made, count(i, p_null_made, NG))
                            last = v.tensor_copy(den_t[:, GH * g:GH * g + GH, :].rearrange("p h n -> p n h"), d[:, :, :, g])
                        last.then_inc(drained(stp), 1)
                        dve.wait_ge(drained(stp), after(i, stp))
                        v.tensor_tensor(den_t[:], den_t[:], p_null[:], ALU.add).then_inc(dve_chain, 1)
                        dve.wait_ge(dve_chain, count(i, dve_chain, next(chained)))
                        v.reciprocal(rec[:], den_t[:]).then_inc(dve_chain, 1)
                        dve.wait_ge(dve_chain, count(i, dve_chain, next(chained)))
                        rt = rt_in[:]
                        v.tensor_copy(rt[:, :, 0:H].bitcast(F32R), rec[:].rearrange("p h n -> p n h")).then_inc(dve_chain, 1)
                        dve.wait_ge(dve_chain, count(i, dve_chain, next(chained)))
                        v.tensor_tensor(rt[:, :, H:2 * H], rec[:].rearrange("p h n -> p n h"), rt[:, :, 0:H], ALU.subtract)
                        v.tensor_tensor(rt[:, :, 2 * H:3 * H], rec[:].rearrange("p h n -> p n h"),
                                                     p_null[:].rearrange("p h n -> p n h"), ALU.mult).then_inc(rt_made, 1)
                    elif kind == "norm":
                        dve.wait_ge(filled(stp), nth(i, stp))
                        ps = bank(stp)
                        if stp[1] == 0:
                            dve.wait_ge(drained("av0", H // 2 - 1), after(i, "av0", H // 2 - 1))
                        v.tensor_tensor(o0[:, stp[1], :], ps[:], o0[:, stp[1], :], ALU.mult).then_inc(drained(stp), 1)
                    elif kind == "out0":
                        dve.wait_ge(filled(stp), nth(i, stp))
                        ps = bank(stp)
                        dve.wait_ge(drained("down"), after(i, "down"))
                        v.scalar_tensor_tensor(gated[:], gated[:], 0.5, ps[:], ALU.mult, ALU.mult).then_inc(drained(stp), 1)
                        dve.wait_ge(drained(stp), after(i, stp))
                        flat = lambda t: t[:].rearrange("p n d -> p (n d)")
                        v.tensor_tensor(flat(x1_t), flat(x_t), gated[:], ALU.add).then_inc(x1_made, 1)
                        dve.wait_ge(x1_made, count(i, x1_made, 1))
                    elif kind == "v1":
                        dve.wait_ge(filled(stp), nth(i, stp))
                        ps = bank(stp)
                        for n in range(NB):
                            last = v.tensor_tensor(v1[:, n, :, 0:D1], ps[:, P * n:P * n + P].rearrange("p (h d) -> p h d", h=H),
                                                   R("bv").rearrange("p (h d) -> p h d", h=H), ALU.add)
                        last.then_inc(drained(stp), 1)
                    elif kind == "s1":
                        dve.wait_ge(lead_made, count(i, lead_made, lead_of[stp]))
                        ps = bank(stp)
                        v.scalar_tensor_tensor(s_parts[M1:P, :], ps[M1:P, :], R("bin")[M1:P], s_parts[M1:P, :].bitcast(F32),
                                                     ALU.add, ALU.subtract).then_inc(drained(stp), 1)
                    elif kind == "ffo":
                        dve.wait_ge(filled(stp), nth(i, stp))
                        ps = bank(stp)
                        for n in range(NB):
                            last = v.tensor_tensor(f1[:, P * n:P * n + P], ps[:, P * n:P * n + P], R("bout"), ALU.add)
                        last.then_inc(drained(stp), 1)
                    elif kind == "tr":
                        n = stp[1]
                        dve.wait_ge(filled(stp), nth(i, stp))
                        ps = bank(stp)[:].rearrange("p (g j c) -> p g j c", g=NG, j=GH)
                        v.reciprocal(rec1[:, n % 2, :].rearrange("p (g j) -> p g j", g=NG), ps[:, :, :, D1]).then_inc(dve_chain, 1)
                        dve.wait_ge(dve_chain, count(i, dve_chain, next(chained)))
                        a = att[:, n].rearrange("p (g j) d -> p g j d", g=NG)
                        for g in range(NG):
                            last = v.tensor_tensor(a[:, g], ps[:, g, :, 0:D1],
                                                   rec1[:, n % 2, GH * g:GH * g + GH].unsqueeze(2).broadcast_to([P, GH, D1]), ALU.mult)
                        last.then_inc(drained(stp), 1)
                    elif kind == "proj":
                        dve.wait_ge(th_made, count(i, th_made, NHID + 2))
                        v.scalar_tensor_tensor(gated[:], ffn_th[:], 1.0, f1[:], ALU.add, ALU.mult).then_inc(dve_chain, 1)
                        dve.wait_ge(dve_chain, count(i, dve_chain, next(chained)))
                        dve.wait_ge(filled(stp), nth(i, stp))
                        ps = bank(stp)
                        for n in range(NB):
                            last = v.tensor_tensor(att_t[:, P * n:P * n + P], ps[:, P * n:P * n + P], R("bp"), ALU.add)
                        last.then_inc(drained(stp), 1)
                        dve.wait_ge(drained(stp), after(i, stp))
                        v.scalar_tensor_tensor(gated[:], gated[:], 0.5, att_t[:], ALU.mult, ALU.mult).then_inc(dve_chain, 1)
                        dve.wait_ge(dve_chain, count(i, dve_chain, next(chained)))
                        dve.wait_ge(out_stored, count(i, out_stored, 0))
                        v.tensor_tensor(out_t[:].rearrange("p n d -> p (n d)"), x1_t[:].rearrange("p n d -> p (n d)"),
                                                      gated[:], ALU.add).then_inc(out_made, 1)

        @block.tensor
        def _(pe):
            mm = nc.tensor.matmul

            pe.wait_ge(loads, 16 * 7)
            for p in range(H // 2):
                last = mm(banks[0][:, 0:P], stage2[:, P * p:P * p + P], wout[:, p, :], start=p == 0, stop=p == H // 2 - 1)
            last.then_inc(setup_p, 1)
            pe.wait_ge(setup_v, 1)
            pe.wait_ge(setup_g, 8)

            with pe.Fori(0, B) as i:
                def three(ps, w_lead, w_rest, x_l, x_r):
                    mm(ps, w_lead, x_l, start=True, stop=False)
                    mm(ps, w_rest, x_l, start=False, stop=False)
                    return mm(ps, w_lead, x_r, start=False, stop=True)

                for stp in steps:
                    kind = stp[0]
                    if kind == "xt":
                        pe.wait_ge(xn_made, count(i, xn_made, stp[1] + 1))
                        pe.wait_ge(drained(stp), nth(i, stp))
                        ps = bank(stp)
                        for n in range(NB):
                            last = nc.tensor.transpose(ps[:, P * n:P * n + P], xn[:, n, :], ident)
                        last.then_inc(filled(stp), 1)
                    elif kind == "kv":
                        pe.wait_ge(drained("xt", 0), after(i, "xt", 0))
                        pe.wait_ge(drained(stp), nth(i, stp))
                        ps = bank(stp)
                        mm(ps[:], R("wkv"), xf[:], start=True, stop=True).then_inc(filled(stp), 1)
                    elif kind == "vs":
                        pe.wait_ge(drained(stp), nth(i, stp))
                        ps = bank(stp)
                        for n in range(NB):
                            last = mm(ps[:, P * n:P * n + P], xf[:, P * n:P * n + P], R("vs"), start=True, stop=True)
                        last.then_inc(filled(stp), 1)
                    elif kind == "prep0":
                        h = stp[1]
                        pe.wait_ge(drained(stp), nth(i, stp))
                        three(bank(stp)[:], wq_lead[:, h], wq_rest[:, h], x_lead[:], x_rest[:]).then_inc(filled(stp), 1)
                    elif kind == "prep1":
                        g = stp[1]
                        if g == 0:
                            pe.wait_ge(drained("xt", 1), after(i, "xt", 1))
                        for n, which in enumerate("qk"):
                            name = ("prep1", which, g)
                            pe.wait_ge(drained(name), nth(i, name))
                            three(bank(name)[:], qk_lead[:, n, g], qk_rest[:, n, g], x_lead[:], x_rest[:]).then_inc(filled(name), 1)
                    elif kind == "sm":
                        layer, h = stp[1:]
                        if layer == 0:
                            if h == 0:
                                pe.wait_ge(drained("kv"), after(i, "kv"))
                            pe.wait_ge(drained("prep0", h), after(i, "prep0", h))
                            q, k = q_two[:, h % (2 * GH), :], k_lead[:]
                        else:
                            g, j = h // GH, h % GH
                            pe.wait_ge(drained("prep1", "q", g), after(i, "prep1", "q", g))
                            pe.wait_ge(k1_spread, count(i, k1_spread, GH * (g + 1)))
                            q, k = q1_st[:, g % 2, :], k1_head[:, h % (2 * GH), :]
                        for u, blocks in enumerate(((3,), (2, 0), (1,))):
                            pe.wait_ge(drained(stp + (u,)), nth(i, stp + (u,)))
                            ps = bank(stp + (u,))
                            for qb in blocks:
                                w, at = P * (qb + 1), (384 if qb == 0 else 0)
                                last = mm(ps[:, at:at + w], q[:, P * qb:P * qb + P], k[:, 0:w], start=True, stop=True)
                            last.then_inc(filled(stp + (u,)), 1)
                    elif kind == "mt":
                        layer, g = stp[1:]
                        pe.wait_ge(parts_made, count(i, parts_made, NG * layer + g + 1))
                        pe.wait_ge(drained(stp), nth(i, stp))
                        ps = bank(stp)
                        nc.tensor.transpose(ps[0:2 * GH * NB, 0:P], max_parts[:, g % 2, :], ident).then_inc(filled(stp), 1)
                    elif kind == "st":
                        layer, h = stp[1:]
                        if h % GH == 0:
                            g = h // GH
                            if layer == 0:
                                pe.wait_ge(y_top, count(i, y_top, g + 1))
                                pe.wait_ge(y_rows, count(i, y_rows, g + 1))
                            else:
                                pe.wait_ge(q1_rows, count(i, q1_rows, GH * (g + 1)))
                        for u, blocks in enumerate(((0,), (1, 3), (2,))):
                            pe.wait_ge(drained(stp + (u,)), nth(i, stp + (u,)))
                            ps = bank(stp + (u,))
                            for kb in blocks:
                                at = KOFF[kb] % T
                                o = ps[:, at:at + kw(kb)]
                                ks, qs = slice(P * kb, P * kb + P), slice(P * kb, T)
                                mm(o[:, 0:P], maskk_b[:], ident_b[:], start=True, stop=False, skip_group_check=True)
                                if layer == 0:
                                    mm(o, k_lead[:, ks], q_two[:, h % (2 * GH), qs], start=False, stop=False, skip_group_check=True)
                                    last = mm(o, k_rest[:, ks], q_max[:, h % (2 * GH), qs], start=False, stop=True, skip_group_check=True)
                                else:
                                    last = mm(o, k1_head[:, h % (2 * GH), ks], q1_max[:, (h // GH) % 2, qs], start=False, stop=True,
                                              skip_group_check=True)
                            last.then_inc(filled(stp + (u,)), 1)
                    elif kind == "gate" or kind == "up":
                        n = 0 if kind == "gate" else 1
                        pe.wait_ge(drained(stp), nth(i, stp))
                        three(bank(stp)[:], wgu_lead[:, n, stp[1]], wgu_rest[:, n, stp[1]], x_lead[:], x_rest[:]).then_inc(filled(stp), 1)
                    elif kind == "down":
                        pe.wait_ge(drained("up", NHID - 1), after(i, "up", NHID - 1))
                        pe.wait_ge(drained(stp), nth(i, stp))
                        ps = bank(stp)
                        for n in range(NB):
                            for c in range(NHID):
                                last = mm(ps[:, P * n:P * n + P], hidden[:, c, P * n:P * n + P], wdown[:, c], start=c == 0, stop=c == NHID - 1)
                        last.then_inc(filled(stp), 1)
                    elif kind == "av0":
                        p = stp[1]
                        pe.wait_ge(drained("st", 0, 2 * p + 1, 2), after(i, "st", 0, 2 * p + 1, 2))
                        if p == 0:
                            pe.wait_ge(drained("vs"), after(i, "vs"))
                        pe.wait_ge(drained(stp), nth(i, stp))
                        ps = bank(stp)
                        for kb in range(NB):
                            for c in range(2):
                                pr = probs[:, (2 * p + c) % GH, KOFF[kb]:KOFF[kb] + kw(kb)]
                                last = mm(ps[D0 * c:D0 * c + D0, P * kb:T], v0[:, kb, :], pr, start=kb == 0, stop=kb == NB - 1,
                                          skip_group_check=True)
                        last.then_inc(filled(stp), 1)
                    elif kind == "den":
                        g = stp[1]
                        if g == 0:
                            pe.wait_ge(drained("den"), nth(i, "den"))
                        ps = bank("den")
                        for kb in range(NB):
                            for j in range(GH):
                                pr = probs[:, j, KOFF[kb]:KOFF[kb] + kw(kb)]
                                last = mm(ps[32 * j:32 * j + 32, P * kb:T], R("onehot")[:, 32 * g:32 * g + 32], pr,
                                          start=kb == 0 and g == 0, stop=kb == NB - 1 and g == NG - 1, skip_group_check=True)
                        if g < NG - 1:
                            last.then_inc(probs_used, 1)
                        else:
                            last.then_inc(filled("den"), 1)
                    elif kind == "lt":
                        pe.wait_ge(drained("den"), after(i, "den"))
                        pe.wait_ge(drained(stp), nth(i, stp))
                        ps = bank(stp)
                        for n in range(NB):
                            last = nc.tensor.transpose(ps[:, P * n:P * n + P], den_s[:, P * n:P * n + P], ident)
                        last.then_inc(filled(stp), 1)
                    elif kind == "rt":
                        pe.wait_ge(rt_made, count(i, rt_made, 1))
                        pe.wait_ge(drained(stp), nth(i, stp))
                        ps = bank(stp)
                        for n in range(NB):
                            last = nc.tensor.transpose(ps[:, P * n:P * n + P], rt_in[:, n, :], ident)
                        last.then_inc(filled(stp), 1)
                    elif kind == "norm":
                        if stp[1] == 0:
                            pe.wait_ge(drained("rt"), after(i, "rt"))
                        pe.wait_ge(drained(stp), nth(i, stp))
                        mm(bank(stp)[:], sel[:, stp[1]], rt_r[:], start=True, stop=True).then_inc(filled(stp), 1)
                    elif kind == "out0":
                        pe.wait_ge(drained("norm", H // 2 - 2), after(i, "norm", H // 2 - 2))
                        pe.wait_ge(drained("norm", H // 2 - 1), after(i, "norm", H // 2 - 1))
                        pe.wait_ge(drained(stp), nth(i, stp))
                        ps = bank(stp)
                        for n in range(NB):
                            c = slice(P * n, P * n + P)
                            for p in range(H // 2):
                                mm(ps[:, c], o0[:, p, c], wout[:, p, :], start=p == 0, stop=False)
                            last = mm(ps[:, c], rt_f[:, c], null_out[:], start=False, stop=True)
                        last.then_inc(filled(stp), 1)
                    elif kind == "v1":
                        pe.wait_ge(drained(stp), nth(i, stp))
                        ps = bank(stp)
                        for n in range(NB):
                            last = mm(ps[:, P * n:P * n + P], xf[:, P * n:P * n + P], R("wv"), start=True, stop=True)
                        last.then_inc(filled(stp), 1)
                    elif kind == "s1":
                        pe.wait_ge(drained(stp), nth(i, stp))
                        mm(bank(stp)[:], R("win"), xf[:], start=True, stop=True).then_inc(filled(stp), 1)
                    elif kind == "ex":
                        if stp[1] == 0:
                            pe.wait_ge(drained("s1"), after(i, "s1"))
                        pe.wait_ge(drained(stp), nth(i, stp))
                        mm(bank(stp)[:], spread[:, stp[1]], s_parts[:], start=True, stop=True).then_inc(filled(stp), 1)
                    elif kind == "con":
                        pe.wait_ge(drained("ex", NE - 2), after(i, "ex", NE - 2))
                        pe.wait_ge(drained("ex", NE - 1), after(i, "ex", NE - 1))
                        pe.wait_ge(drained(stp), nth(i, stp))
                        ps = bank(stp)
                        for n in range(NE):
                            j = n % 4
                            last = mm(ps[32 * j:32 * j + 32, :], R("w2")[:, 32 * n:32 * n + 32], pieces[:, n, :],
                                      start=n < 4, stop=n >= 4, skip_group_check=True)
                        last.then_inc(filled(stp), 1)
                    elif kind == "ffo":
                        pe.wait_ge(drained("con"), after(i, "con"))
                        pe.wait_ge(drained(stp), nth(i, stp))
                        ps = bank(stp)
                        for n in range(NB):
                            last = mm(ps[:, P * n:P * n + P], g1[:, P * n:P * n + P], R("wo1"), start=True, stop=True)
                        last.then_inc(filled(stp), 1)
                    elif kind == "av1":
                        g = stp[1]
                        pe.wait_ge(drained("st", 1, GH * g + 3, 2), after(i, "st", 1, GH * g + 3, 2))
                        if g == 0:
                            pe.wait_ge(drained("v1"), after(i, "v1"))
                        pe.wait_ge(drained(stp), nth(i, stp))
                        ps = bank(stp)
                        for kb in range(NB):
                            for j in range(GH):
                                pr = probs[:, j, KOFF[kb]:KOFF[kb] + kw(kb)]
                                last = mm(ps[32 * j:32 * j + 32, P * kb:T], v1[:, kb, GH * g + j, :], pr, start=kb == 0, stop=kb == NB - 1,
                                          skip_group_check=True)
                        last.then_inc(filled(stp), 1)
                    elif kind == "tr":
                        n = stp[1]
                        if n == 0:
                            pe.wait_ge(drained("av1", NG - 1), after(i, "av1", NG - 1))
                        pe.wait_ge(drained(stp), nth(i, stp))
                        ps = bank(stp)
                        for g in range(NG):
                            last = nc.tensor.transpose(ps[:, P * g:P * g + P], o1[:, g, P * n:P * n + P], ident)
                        last.then_inc(filled(stp), 1)
                    elif kind == "att":
                        pe.wait_ge(drained("tr", NB - 2), after(i, "tr", NB - 2))
                        pe.wait_ge(drained("tr", NB - 1), after(i, "tr", NB - 1))
                        pe.wait_ge(drained(stp), nth(i, stp))
                        ps = bank(stp)
                        for n in range(NB):
                            last = nc.tensor.transpose(ps[:, P * n:P * n + P], att[:, n].rearrange("p h d -> p (h d)"), ident)
                        last.then_inc(filled(stp), 1)
                    elif kind == "proj":
                        pe.wait_ge(drained("att"), after(i, "att"))
                        pe.wait_ge(drained(stp), nth(i, stp))
                        ps = bank(stp)
                        for n in range(NB):
                            last = mm(ps[:, P * n:P * n + P], att_t[:, P * n:P * n + P], R("wp"), start=True, stop=True)
                        last.then_inc(filled(stp), 1)


def kernel(L0_attn_x, L0_attn_Wq, L0_attn_Wkv, L0_attn_null_kv, L0_attn_Wout, L0_ffn_w_gate, L0_ffn_w_up, L0_ffn_w_down,
           L1_attn_W_qkv, L1_attn_b_qkv, L1_attn_W_proj, L1_attn_b_proj, L1_ffn_Win, L1_ffn_bin_, L1_ffn_W1, L1_ffn_b1,
           L1_ffn_W2, L1_ffn_b2, L1_ffn_Wout, L1_ffn_bout):
    import concourse.bacc as bacc
    from concourse.bass_utils import run_bass_kernel_spmd

    f = np.float32
    a = lambda v: np.asarray(v)
    rows = lambda v: np.broadcast_to(a(v).reshape(1, -1), (P, a(v).size))
    part = np.arange(P)

    ident = np.eye(P, dtype=f)
    maskq = np.zeros((P, T), f)
    maskq[:, T - P:] = np.where(part[None, :] > part[:, None], f(NEG), f(0))
    maskk = np.where(part[None, :] > part[:, None], f(NEG), f(0)).astype(f)
    onehot = np.zeros((P, NG, 32), f)
    for g in range(NG):
        onehot[:, g, g::4] = 1
    lowmask = np.zeros((P, 3), f)
    lowmask[D0:, 0] = 1
    lowmask[part % 32 // D1 == 1, 1] = 1
    lowmask[part % 32 // D1 == 2, 2] = 1
    sel = np.zeros((P, H // 2, P), f)
    for h in range(H):
        sel[[h, H + h], h // 2, D0 * (h % 2):D0 * (h % 2) + D0] = 1
    spread = np.zeros((P, NE, P), f)
    for m in range(M1):
        c = IN1 * (m % (P // IN1))
        spread[[m, M1 + m], m // (P // IN1), c:c + IN1] = 1

    wq = a(L0_attn_Wq).reshape(D, H, 1, D0)
    wq2 = np.concatenate([wq, wq], axis=2).reshape(D, H * P)
    wkv = a(L0_attn_Wkv)
    vs = np.zeros((P, P), f)
    vs[:, 0:D0] = wkv
    nullsel = np.zeros((P, H // 2, P), f)
    for h in range(H):
        nullsel[D0 * (h % 2):D0 * (h % 2) + D0, h // 2, 2 * H + h] = a(L0_attn_null_kv)

    w3 = a(L1_attn_W_qkv).reshape(D, 3, NG, GH, D1)
    b3 = a(L1_attn_b_qkv).reshape(3, NG, GH, D1)
    qk = np.zeros((D, 2, NG, GH, 32), f)
    bqk = np.zeros((GH, 32, 2, NG), f)
    bqk_low = np.zeros((GH, 32, 2, NG), f)
    for n in range(2):
        for r in range(3):
            qk[:, n, :, :, D1 * r:D1 * r + D1] = w3[:, n]
            bqk[:, D1 * r:D1 * r + D1, n] = b3[n].transpose(1, 2, 0)
        bqk_low[:, D1 * (n + 1):D1 * (n + 2), n] = b3[n].transpose(1, 2, 0)
    bqk[:, 3 * D1:3 * D1 + 2, 1] = -1
    w2 = np.zeros((P, NE, 32), f)
    wo1 = np.zeros((P, D), f)
    b2 = np.zeros((P, 1), f)
    mt = P // IN1
    for m in range(M1):
        e, ml = m // mt, m % mt
        w2[IN1 * ml:IN1 * ml + IN1, e, mt * (e // 4) + ml] = a(L1_ffn_W2)[m]
        row = 32 * (e % 4) + mt * (e // 4) + ml
        wo1[row] = a(L1_ffn_Wout)[m]
        b2[row] = a(L1_ffn_b2)[m]
    two = lambda v: np.concatenate([v, v], axis=1)
    col = lambda v: a(v).reshape(NE, P).T
    packed = {
        "ident": ident, "wkv": two(wkv), "vs": vs, "maskq": maskq, "maskk": maskk, "onehot": onehot.reshape(P, -1),
        "lowmask": lowmask, "bqk": bqk.reshape(P, -1), "bqk_low": bqk_low.reshape(P, -1),
        "wv": a(L1_attn_W_qkv)[:, 2 * D:], "bv": rows(a(L1_attn_b_qkv)[2 * D:]), "wp": a(L1_attn_W_proj), "bp": rows(L1_attn_b_proj),
        "win": two(a(L1_ffn_Win)), "bin": two(a(L1_ffn_bin_).reshape(1, -1)).T, "w1": col(L1_ffn_W1), "b1": col(L1_ffn_b1),
        "w2": w2.reshape(P, -1), "b2": b2, "wo1": wo1, "bout": rows(L1_ffn_bout),
    }
    arrays = {
        "x": a(L0_attn_x),
        "res": np.ascontiguousarray(np.concatenate([packed[n] for n in RES], axis=1)),
        "stg": np.ascontiguousarray(np.concatenate([wq2, qk.reshape(D, -1), sel.reshape(P, -1), spread.reshape(P, -1)], axis=1)),
        "st2": np.ascontiguousarray(np.concatenate([nullsel.reshape(P, -1), rows(L0_attn_null_kv)], axis=1)),
        "wout": a(L0_attn_Wout),
        "wg": np.ascontiguousarray(a(L0_ffn_w_gate).T),
        "wu": np.ascontiguousarray(a(L0_ffn_w_up).T),
        "wd": np.ascontiguousarray(a(L0_ffn_w_down).T),
    }
    nc = bacc.Bacc("TRN2", target_bir_lowering=False, num_devices=1)
    aps = [nc.dram_tensor(f"{n}_dram", v.shape, mybir.dt.from_np(v.dtype), kind="ExternalInput").ap() for n, v in arrays.items()]
    out = nc.dram_tensor("out", (B, T, D), F32, kind="ExternalOutput").ap()
    two_layers(nc, *aps, out)
    r = run_bass_kernel_spmd(nc, [{f"{n}_dram": v for n, v in arrays.items()}], core_ids=[0])
    return r.results[0]["out"]
```

```python
from contextlib import ExitStack

import numpy as np

import concourse.bass as bass
from concourse import mybir

F32 = mybir.dt.float32
F32R = mybir.dt.float32r
BF16 = mybir.dt.bfloat16
I32 = mybir.dt.int32
ALU = mybir.AluOpType
ACT = mybir.ActivationFunctionType

P = 128
B, T, D = 16, 512, 128
NB = T // P
H = 16
NG = 4
GH = H // NG
D0 = 64
D1 = D // H
HID = 384
NHID = HID // P
M1, IN1 = 64, 16
NE = M1 * IN1 // P
EPS = 1e-5
CHAIN = (10, 15)
RING = 6
NEG = -1e30
DEQ = 1.0 / 127.0

RES = {}
_at = 0
for _name, _n in [("ident", P), ("wkv", P), ("vs", P), ("maskq", T), ("maskk", P), ("onehot", NG * 32), ("lowmask", 3),
                  ("bqk", 2 * NG), ("bqk_low", 2 * NG), ("wv", P), ("bv", P), ("wp", P), ("bp", P), ("win", P),
                  ("bin", 1), ("w1", NE), ("b1", NE), ("w2", NE * 32), ("b2", 1), ("wo1", P), ("bout", P)]:
    RES[_name] = (_at, _at + _n)
    _at += _n
NRES = _at
STG = {"wq": (0, 2048), "qk": (2048, 3072), "sel": (3072, 4096), "exp": (4096, 5120)}
NSTG = 5120
ST2 = {"nullsel": (0, 1024), "null": (1024, 1088)}
NST2 = 1088

KOFF = (0, 512, 1024, 896)


def kw(kb):
    return T - P * kb


ROOM = {"ln0": 2, "xt0": 2, "kv": 1, "vs": 1, "prep0": 0.8, "sm0": 0.6, "st0": 0.6, "gate": 1, "up": 1, "down": 3, "max0": 1,
        "mt0": 0.5, "av0": 1, "den": 2.5, "denc": 1,
        "lt": 3, "rt": 2, "norm": 1, "out0": 1, "ln1": 6, "xt1": 3, "prep1": 3, "v1": 2, "s1": 2, "ex": 1, "con": 1, "ffo": 2,
        "sm1": 0.6, "st1": 0.6, "max1": 1, "mt1": 1, "av1": 1, "tr": 1, "att": 2, "proj": 2}
UNTIL = 0.97


def room(stp):
    return ROOM[stp[0]] if stp[0] in ROOM else ROOM[f"{stp[0]}{stp[1]}"]


def units(layer, *heads):
    return [(kind, layer, h, u) for u in range(3) for kind, h in heads]


def spread_over(a, b, until):
    at = []
    for which, steps, end in ((0, a, 1), (1, b, until)):
        t, total = 0, sum(room(stp) for stp in steps)
        for stp in steps:
            at.append((t / total * end, which, len(at), stp))
            t += room(stp)
    return [stp for *_, stp in sorted(at)]


def first_half():
    s = [("ln", 0), ("xt", 0), ("kv",), ("vs",), ("prep0", 0), ("prep0", 1), ("prep0", 2)]
    s += units(0, ("sm", 0)) + [("prep0", 3), ("gate", 0), ("up", 0)]
    s += units(0, ("sm", 1)) + [("gate", 1), ("up", 1)]
    s += units(0, ("sm", 2)) + [("gate", 2), ("up", 2)] + units(0, ("sm", 3))
    s += [("max", 0, 0), ("down",), ("mt", 0, 0), ("prep0", 4), ("prep0", 5)]
    for g in range(NG):
        h, p, more = GH * g, GH * g // 2, g + 1 < NG
        a = units(0, ("st", h), ("st", h + 1)) + [("av0", p, 0), ("av0", p, 1)] + units(0, ("st", h + 2), ("st", h + 3))
        if more:
            b = units(0, ("sm", h + 4)) + [("prep0", h + 6)] + units(0, ("sm", h + 5)) + [("prep0", h + 7)]
            a = spread_over(a, b + units(0, ("sm", h + 6)) + units(0, ("sm", h + 7)), 1) + [("max", 0, g + 1)]
        s += a + [("av0", p + 1, 0), ("av0", p + 1, 1)]
        if more:
            s += [("mt", 0, g + 1)]
        if g + 2 < NG:
            s += [("prep0", h + 8)]
        s += [("den", g)]
        if g + 2 < NG:
            s += [("prep0", h + 9)]
    return s + [("denc",)]


def second_half():
    s = [("lt",), ("rt",), ("norm", 0)]
    for p in range(1, H // 2):
        s += [("norm", p), ("out0", p - 1)]
    s += [("out0", H // 2 - 1), ("ln", 1), ("xt", 1)]
    s += [("prep1", 0), ("v1",), ("s1",), ("ex", 0), ("ex", 1)] + units(1, ("sm", 0))
    s += [("ex", 2), ("ex", 3)] + units(1, ("sm", 1)) + [("con", 0), ("ex", 4), ("ex", 5)]
    s += units(1, ("sm", 2)) + [("ex", 6), ("ex", 7)] + units(1, ("sm", 3))
    s += [("max", 1, 0), ("con", 1), ("mt", 1, 0), ("prep1", 1), ("ffo",)]
    for g in range(NG):
        h, n, more = GH * g, GH * g + GH, g + 1 < NG
        s += units(1, ("st", h))
        if more:
            s += units(1, ("st", h + 1), ("sm", n)) + units(1, ("st", h + 2), ("sm", n + 1), ("sm", n + 2)) + units(1, ("sm", n + 3))
            s += [("max", 1, g + 1)] + units(1, ("st", h + 3)) + [("mt", 1, g + 1)]
        else:
            s += units(1, ("st", h + 1)) + units(1, ("st", h + 2)) + units(1, ("st", h + 3))
        if g + 2 < NG:
            s += [("prep1", g + 2)]
        s += [("av1", g, 0), ("av1", g, 1)]
    return s + [("tr", n) for n in range(NB)] + [("att",), ("proj",)]


def merged(first, second):
    order = spread_over(first, second, UNTIL)
    kept = []
    while order:
        stp = order.pop(0)
        kept.append(stp)
        if stp[0] in ("av0", "av1") and stp[2] == 0:
            end = order.index(stp[:2] + (1,))
            beside = [x for x in order[:end] if x[0] in ("st", "sm", "ln", "max", "out0", "den")]
            held = [x for x in order[:end] if x not in beside]
            order[:end + 1] = beside + [stp[:2] + (1,)] + held
    order = kept
    for one, other in ((("lt",), ("gate", 0)), (("out0", H // 2 - 1), ("down",)), (("out0", H // 2 - 1), ("den", 0)), (("down",), ("ex", 0)), (("vs",), ("xt", 1)),
                       (("xt", 0), ("ln", 1)), (("lt",), ("max", 0, 0)), (("proj",), ("denc",))):
        assert order.index(one) < order.index(other), (one, other)
    return order


def bank_plan(steps):
    uses, order = [0] * 8, {}
    turns = {"st": 0, "sm": 0, "any": 0}

    def take(name, pool):
        if pool == "st":
            bank = turns[pool] % 2
        elif pool == "sm":
            bank = 2 + turns[pool] % 3
        elif pool == "any":
            bank = 5 + turns[pool] % 2
        else:
            bank = 7
        if pool in turns:
            turns[pool] += 1
        order[name] = (bank, uses[bank])
        uses[bank] += 1

    for st in steps:
        kind = st[0]
        if kind in ("st", "sm"):
            take(st, kind)
        elif kind == "prep1":
            take(("prep1", "q", st[1]), "any")
            take(("prep1", "k", st[1]), "any")
        elif kind in ("den", "out0"):
            if st[1] == 0:
                take((kind,), "sums")
        elif kind in ("av0", "av1"):
            if st[2] == 0:
                take(st[:2], "any")
        elif kind not in ("ln", "max", "denc"):
            take(st, "any")
    return order, uses


class Trip:

    def __init__(self, steps, full, banks, bank_filled, bank_drained):
        self.steps = steps
        self.unit, self.uses = bank_plan(steps)
        self.full, self.banks, self.bank_filled, self.bank_drained = full, banks, bank_filled, bank_drained
        self.missing = [0] * 8

    def _before(self, i, b):
        return 0 if isinstance(i, int) and i == 0 else i * self.full[b] - self.missing[b]

    def _plan(self, name):
        return self.unit[name[0] if isinstance(name[0], tuple) else name]

    def has(self, *name):
        return name in self.unit

    def bank(self, *name):
        return self.banks[self._plan(name)[0]]

    def filled(self, *name):
        return self.bank_filled[self._plan(name)[0]]

    def drained(self, *name):
        return self.bank_drained[self._plan(name)[0]]

    def nth(self, i, *name):
        b, k = self._plan(name)
        return self._before(i, b) + (k + 1)

    def after(self, i, *name):
        b, k = self._plan(name)
        return self._before(i, b) + (k + 2)

    def distinct(self, own, *names):
        last = {}
        for name in names:
            b, k = self.unit[name]
            if b != (self.unit[own][0] if own else None) and k >= self.unit[last.get(b, name)][1]:
                last[b] = name
        return last.values()

    def earlier(self, i, b):
        return self._before(i, b) + 1


def two_layers(nc, x_d, res_d, stg_d, st2_d, wout_d, wg_d, wu_d, wd_d, out_d):
    with ExitStack() as ctx:
        def sb(name, shape, dt=F32):
            return ctx.enter_context(nc.sbuf_tensor(name, shape, dt))

        def sem(name):
            return ctx.enter_context(nc.semaphore(name))

        res = sb("res", [P, NRES])
        wq_lead, wq_rest = sb("wq_lead", [P, H, P], F32R), sb("wq_rest", [P, H, P], F32R)
        wgu_lead, wgu_rest = sb("wgu_lead", [P, 2, NHID, P], F32R), sb("wgu_rest", [P, 2, NHID, P], F32R)
        qk_lead, qk_rest = sb("qk_lead", [P, 2, NG, P], F32R), sb("qk_rest", [P, 2, NG, P], F32R)
        sel = sb("sel", [P, H // 2, P], F32R)
        spread = sb("spread", [P, NE, P], F32R)
        wout = sb("wout", [P, H // 2, P])
        wdown = sb("wdown", [P, NHID, P])
        null_out = sb("null_out", [P, P])
        ident_b, maskk_b = sb("ident_b", [P, P], BF16), sb("maskk_b", [P, P], BF16)
        half_neg = sb("half_neg", [P, NB])

        x_t, xn = sb("x_t", [P, NB, D]), sb("xn", [P, NB, D])
        x1_t = sb("x1_t", [P, NB, D])
        stats, mv, var_e, rstd = sb("stats", [P, NB, 6]), sb("mv", [P, NB, 2]), sb("var_e", [P, NB]), sb("rstd", [P, NB])
        xf = sb("xf", [P, T])
        x_lead, x_rest = (sb("x0_lead", [P, T], F32R), sb("x1_lead", [P, T], F32R)), (sb("x0_rest", [P, T], F32R), sb("x1_rest", [P, T], F32R))
        k_lead, k_rest = sb("k_lead", [P, T], F32R), sb("k_rest", [P, T], F32R)
        v0, s_null = sb("v0", [P, NB, D0]), sb("s_null", [P, H, NB])
        cut, cut1 = sb("cut", [P, 2, T], F32R), sb("cut1", [P, T], F32R)
        q_two, q_max = sb("q_two", [P, RING, T], F32R), sb("q_max", [P, RING, T], F32R)
        q1_st, k1_st = sb("q1_st", [P, 2, T], F32R), sb("k1_st", [P, T], F32R)
        k1_head = sb("k1_head", [P, 2 * GH, T], F32R)
        o0, o1 = sb("o0", [P, H // 2, T]), sb("o1", [P, NG, T])
        probs = sb("probs0", [P, GH, 1280]), sb("probs1", [P, GH, 1280])
        v1 = sb("v1", [P, NB, H * (D1 + 1) + 32 - (D1 + 1)])
        rowmax = sb("rowmax0", [P, GH, NB]), sb("rowmax1", [P, GH, NB])
        max_parts = sb("max_parts0", [P, 2, 2 * GH * NB]), sb("max_parts1", [P, 2, 2 * GH * NB])
        max_t = sb("max_t0", [2 * GH * NB, 2, P], F32R), sb("max_t1", [2 * GH * NB, 2, P], F32R)
        p_arg, p_null = sb("p_arg", [P, H, NB]), sb("p_null", [P, H, NB])
        den_s = sb("den_s", [P, T])
        den_t, rec = sb("den_t", [P, H, NB]), sb("rec", [P, H, NB])
        rt_in = sb("rt_in", [P, NB, P])
        rt_r, rt_f = cut1, k1_st[:].bitcast(F32)
        gated0, f1 = sb("gated0", [P, T]), sb("f1", [P, T])
        hg, hidden, pieces = f1, o1[:, 0:NHID], o1
        th = att_t = den_s
        s_parts, att = cut1[:], xn[:].rearrange("p n (h d) -> p n h d", h=H)
        g1 = xf
        rec1 = sb("rec1", [P, 2, H])
        banks = [ctx.enter_context(nc.psum_tensor(f"bank{n}", [P, T], F32)) for n in range(8)]
        stage = probs[0][:].rearrange("p h c -> p (h c)")
        stage2 = o0[:].rearrange("p h c -> p (h c)")
        stage_i = o1[:].rearrange("p h c -> p (h c)").bitcast(I32)

        def R(name):
            return res[:, RES[name][0]:RES[name][1]]

        ident = R("ident")

        counts = {}

        def counting(name, per, half=0, step=1, base=0):
            s = sem(name)
            counts[s.name] = per, half, step, base
            return s

        def count(i, s, n):
            per, half, step, base = counts[s.name]
            return i * (per * step) + (n + base - half * per) * step

        bank_filled = [sem(f"bank{n}_filled") for n in range(8)]
        bank_drained = [sem(f"bank{n}_drained") for n in range(8)]
        x_loaded, x_reloaded = counting("x_loaded", 1, 0, 16), counting("x_reloaded", 1, 1, 16)
        out_stored = counting("out_stored", 1, 1, 16, 1)
        var_made = counting("var0_made", 1), counting("var1_made", 1, 1)
        rstd_made = counting("rstd0_made", 1), counting("rstd1_made", 1, 1)
        xn_made = counting("xn0_made", 1), counting("xn1_made", 1, 1)
        x1_made, out_made = counting("x1_made", 1, 1), counting("out_made", 1, 1)
        lead_made = counting("lead0_made", 2 + H), counting("lead1_made", 2 + 2 * NG, 1)
        parts_made = counting("parts0_made", NG), counting("parts1_made", NG, 1)
        q_top = [counting(f"q_top{n}", H // 8, 0, 16) for n in range(4)]
        q_rows = counting("q_rows", H // 2, 0, 16)
        q1_rows, k1_spread = counting("q1_rows", NG * GH, 1, 16), counting("k1_spread", H, 1, 16)
        p_arg_made, p_null_made = counting("p_arg_made", NG), counting("p_null_made", NG)
        probs_used = counting("probs_used", NG)
        rt_made, norms_made = counting("rt_made", 1, 1), counting("norms_made", 1, 1)
        th_made = counting("th0_made", NHID + 1), counting("th1_made", 1, 1)
        dve_chain = counting("dve_chain0", CHAIN[0]), counting("dve_chain1", CHAIN[1], 1)
        passed = sem("passed")
        loads, setup_v, setup_p, setup_g, setup_b = sem("loads"), sem("setup_v"), sem("setup_p"), sem("setup_g"), sem("setup_b")

        first, second = first_half(), second_half()
        both = merged(first, second)
        full = bank_plan(both)[1]
        trips = [Trip(s, full, banks, bank_filled, bank_drained)
                 for s in (first, both, second)]
        for trip in trips:
            trip.missing = [n - k for n, k in zip(full, trips[0].uses)]

        lead_of = {}
        for half in (first, second):
            n = 0
            for stp in half:
                n += {"xt": 1, "kv": 1, "prep0": 1, "s1": 1, "prep1": 2}.get(stp[0], 0)
                lead_of[stp] = n
        cut_at = {}
        for h in range(H):
            cut_at["prep0", h] = h % 2

        block = ctx.enter_context(nc.Block())

        @block.sync
        def _(sp):
            sp.dma_start(res[:], res_d).then_inc(loads, 16)
            sp.dma_start(stage[:, 0:NSTG], stg_d).then_inc(loads, 16)
            sp.dma_start(stage2[:, 0:NST2], st2_d).then_inc(loads, 16)
            sp.dma_start(wout[:], wout_d.rearrange("(c p) n -> p c n", p=P)).then_inc(loads, 16)
            sp.dma_start(stage_i[:, 0:HID], wg_d).then_inc(loads, 16)
            sp.dma_start(stage_i[:, HID:2 * HID], wu_d).then_inc(loads, 16)
            sp.dma_start(stage_i[:, 2 * HID:3 * HID].rearrange("p (c n) -> p c n", c=NHID),
                         wd_d.rearrange("(c p) n -> p c n", p=P)).then_inc(loads, 16)
            xv = x_d.rearrange("b (n p) d -> b p n d", p=P)
            ov = out_d.rearrange("b (n p) d -> b p n d", p=P)
            sp.dma_start(x_t[:], xv[0]).then_inc(x_loaded, 16)
            def trip_sp(i, trip):
                bank, filled, drained, nth, after, earlier = trip.bank, trip.filled, trip.drained, trip.nth, trip.after, trip.earlier
                for stp in trip.steps:
                    kind = stp[0]
                    if kind == "xt" and stp[1] == 0:
                        sp.wait_ge(xn_made[0], count(i, xn_made[0], 1))
                        sp.sem_inc(passed, 1)
                        sp.dma_start(x_t[:], xv[(i + 1) % B]).then_inc(x_loaded, 16)
                    elif kind == "lt":
                        sp.wait_ge(out_stored, count(i, out_stored, 0))
                        sp.sem_inc(passed, 1)
                        sp.dma_start(x1_t[:], xv[i - 1]).then_inc(x_reloaded, 16)
                    elif kind == "prep0" and stp[1] % 2 == 1:
                        h = stp[1] - 1
                        r = h % RING
                        sp.wait_ge(drained("prep0", h + 1), after(i, "prep0", h + 1))
                        sp.sem_inc(passed, 1)
                        if h >= RING:
                            sp.wait_ge(drained("st", 0, h + 1 - RING, 2), after(i, "st", 0, h + 1 - RING, 2))
                            sp.sem_inc(passed, 1)
                        sp.dma_start(q_max[0:D0, r:r + 2, :].bitcast(F32), q_two[0:D0, r:r + 2, :].bitcast(F32)).then_inc(q_top[h // 2 % 4], 16)
                    elif kind == "mt":
                        layer, g = stp[1:]
                        src = max_t[layer][:, g % 2, :].bitcast(F32)
                        sp.wait_ge(drained(stp), after(i, stp))
                        sp.sem_inc(passed, 1)
                        if layer == 0:
                            for e in range(2):
                                r = (GH * g + 2 * e) % RING
                                sp.dma_start(q_max[D0:D0 + 2, r:r + 2, :].bitcast(F32), src[16 * e:16 * e + 16]).then_inc(q_rows, 16)
                        else:
                            for j in range(GH):
                                sp.dma_start(q1_st[32 * j + 24:32 * j + 26, g % 2, :].bitcast(F32),
                                             src[8 * j:8 * j + 8]).then_inc(q1_rows, 16)
                    elif kind == "prep1":
                        g = stp[1]
                        sp.wait_ge(drained("prep1", "k", g), after(i, "prep1", "k", g))
                        sp.sem_inc(passed, 1)
                        if g >= 2:
                            sp.wait_ge(drained("st", 1, GH * (g - 2) + 3, 2), after(i, "st", 1, GH * (g - 2) + 3, 2))
                            sp.sem_inc(passed, 1)
                        for j in range(GH):
                            sp.dma_start(k1_head[32 * j:32 * j + 32, GH * (g % 2) + j, :].bitcast(F32),
                                         k1_st[32 * j:32 * j + 32, :].bitcast(F32)).then_inc(k1_spread, 16)
                    elif kind == "proj":
                        sp.wait_ge(out_made, count(i, out_made, 1))
                        sp.sem_inc(passed, 1)
                        sp.dma_start(ov[i - 1], x1_t[:]).then_inc(out_stored, 16)

            trip_sp(0, trips[0])
            with sp.Fori(1, B) as i:
                trip_sp(i, trips[1])
            trip_sp(B, trips[2])
            sp.wait_ge(out_stored, 16 * (B + 1))
            sp.wait_ge(x_loaded, 16 * (B + 1))

        @block.gpsimd
        def _(pool):
            ones = v1[:, :, 0:H * (D1 + 1)].rearrange("p n (h c) -> p n h c", h=H)[:, :, :, D1]
            for b in range(8):
                pool.sem_inc(bank_drained[b], 1)
            pool.sem_inc(out_stored, 16)
            nc.gpsimd.memset(half_neg[:], -0.5).then_inc(setup_g, 1)
            nc.gpsimd.memset(q_max[:].bitcast(F32), 0.0).then_inc(setup_g, 1)
            nc.gpsimd.memset(k1_head[:].bitcast(F32), 0.0).then_inc(setup_g, 1)
            nc.gpsimd.memset(k_rest[:].bitcast(F32), 0.0).then_inc(setup_g, 1)
            nc.gpsimd.memset(rt_in[:], 0.0).then_inc(setup_g, 1)
            nc.gpsimd.memset(v1[:], 0.0).then_inc(setup_g, 1)
            pool.wait_ge(setup_g, 6)
            nc.gpsimd.memset(k_rest[D0:D0 + 2, :].bitcast(F32), -1.0).then_inc(setup_g, 1)
            pool.wait_ge(setup_g, 7)
            nc.gpsimd.memset(ones, 1.0).then_inc(setup_g, 1)
            pool.wait_ge(setup_g, 8)
            def rstd_of(i, layer):
                pool.wait_ge(var_made[layer], count(i, var_made[layer], 1))
                nc.gpsimd.tensor_tensor(rstd[:], var_e[:], half_neg[:], ALU.pow).then_inc(rstd_made[layer], 1)

            order = [stp[1] for stp in both if stp[0] == "ln"]
            rstd_of(0, 0)
            with pool.Fori(1, B) as i:
                for layer in order:
                    rstd_of(i, layer)
            rstd_of(B, 1)

        @block.scalar
        def _(act):
            def copy(out, in_):
                return nc.scalar.activation(out, in_, ACT.Copy)

            act.wait_ge(loads, 16 * 7)
            act.wait_ge(setup_v, 1)
            act.wait_ge(setup_g, 8)
            def trip_act(i, trip):
                bank, filled, drained, nth, after, earlier = trip.bank, trip.filled, trip.drained, trip.nth, trip.after, trip.earlier
                for stp in trip.steps:
                    kind = stp[0]
                    if kind == "xt":
                        act.wait_ge(filled(stp), nth(i, stp))
                        ps = bank(stp)
                        copy(xf[:], ps[:])
                        copy(x_lead[stp[1]][:], ps[:]).then_inc(lead_made[stp[1]], 1)
                    elif kind == "kv":
                        act.wait_ge(filled(stp), nth(i, stp))
                        ps = bank(stp)
                        copy(k_lead[:], ps[:]).then_inc(lead_made[0], 1)
                    elif kind == "prep0":
                        act.wait_ge(filled(stp), nth(i, stp))
                        ps = bank(stp)
                        h = stp[1]
                        if h >= 2:
                            act.wait_ge(drained("prep0", h - 2), after(i, "prep0", h - 2))
                        nc.scalar.activation(cut[:, cut_at[stp], :], ps[:], ACT.Copy,
                                             scale=R("lowmask")[:, 0:1]).then_inc(lead_made[0], 1)
                    elif kind == "prep1":
                        g = stp[1]
                        for n, which in enumerate("qk"):
                            act.wait_ge(filled("prep1", which, g), nth(i, "prep1", which, g))
                            ps = bank("prep1", which, g)
                            if n == 1:
                                act.wait_ge(drained("prep1", "q", g), after(i, "prep1", "q", g))
                            elif g >= 1:
                                act.wait_ge(drained("prep1", "k", g - 1), after(i, "prep1", "k", g - 1))
                            nc.scalar.activation(cut1[:], ps[:], ACT.Identity,
                                                                scale=R("lowmask")[:, 1 + n:2 + n],
                                                                bias=R("bqk_low")[:, NG * n + g:NG * n + g + 1]).then_inc(lead_made[1], 1)
                    elif kind == "mt":
                        layer, g = stp[1:]
                        act.wait_ge(filled(stp), nth(i, stp))
                        ps = bank(stp)
                        copy(max_t[layer][:, g % 2, :], ps[0:2 * GH * NB, 0:P]).then_inc(drained(stp), 1)
                        if layer == 0:
                            if g == 0 and trip.has("lt"):
                                act.wait_ge(rt_made, count(i, rt_made, 1))
                            act.wait_ge(p_arg_made, count(i, p_arg_made, g + 1))
                            nc.scalar.activation(p_null[:, GH * g:GH * g + GH, :], p_arg[:, GH * g:GH * g + GH, :],
                                                                  ACT.Exp, scale=D0 ** -0.5).then_inc(p_null_made, 1)
                    elif kind == "st":
                        layer, h, u = stp[1:]
                        scale = float(D0 if layer == 0 else D1) ** -0.5
                        if layer == 0 and u == 0 and not (trip is trips[0] and h < GH):
                            act.wait_ge(probs_used, count(i, probs_used, h // GH))
                        elif layer == 1 and u == 0 and h >= GH:
                            act.wait_ge(filled("av1", h // GH - 1), nth(i, "av1", h // GH - 1))
                        pr = probs[layer][:, h % GH, :]
                        a, b = ((0, 512), (512, 1024), (1024, 1280))[u]
                        act.wait_ge(filled(stp), nth(i, stp))
                        ps = bank(stp)
                        nc.scalar.activation(pr[:, a:b], ps[:, 0:b - a], ACT.Exp, scale=scale).then_inc(drained(stp), 1)
                    elif kind == "gate":
                        act.wait_ge(filled(stp), nth(i, stp))
                        ps = bank(stp)
                        if stp[1] >= 1:
                            act.wait_ge(drained("gate", stp[1] - 1), after(i, "gate", stp[1] - 1))
                        nc.scalar.activation(th[:], ps[:], ACT.Tanh, scale=0.5).then_inc(th_made[0], 1)
                    elif kind == "down":
                        act.wait_ge(filled(stp), nth(i, stp))
                        ps = bank(stp)
                        nc.scalar.activation(th[:], ps[:], ACT.Tanh, scale=0.5).then_inc(th_made[0], 1)
                    elif kind == "av0" and stp[2] == 1:
                        p = stp[1]
                        act.wait_ge(filled("av0", p), nth(i, "av0", p))
                        copy(o0[:, p, :], bank("av0", p)[:]).then_inc(drained("av0", p), 1)
                    elif kind == "denc":
                        if trip.has("proj"):
                            act.wait_ge(out_made, count(i, out_made, 1))
                        act.wait_ge(filled("den"), nth(i, "den"))
                        ps = bank("den")
                        copy(den_s[:], ps[:]).then_inc(drained("den"), 1)
                    elif kind == "rt":
                        act.wait_ge(filled(stp), nth(i, stp))
                        ps = bank(stp)
                        copy(rt_r[:], ps[:])
                        copy(rt_f, ps[:]).then_inc(drained(stp), 1)
                    elif kind == "s1":
                        act.wait_ge(filled(stp), nth(i, stp))
                        ps = bank(stp)
                        nc.scalar.activation(s_parts, ps[:], ACT.Identity, bias=R("bin")).then_inc(lead_made[1], 1)
                    elif kind == "ex":
                        n = stp[1]
                        act.wait_ge(filled(stp), nth(i, stp))
                        ps = bank(stp)
                        if n == GH:
                            act.wait_ge(filled("con", 0), nth(i, "con", 0))
                        nc.scalar.activation(pieces[:, n % GH, :], ps[:], ACT.Relu, scale=R("w1")[:, n:n + 1],
                                                   bias=R("b1")[:, n:n + 1]).then_inc(drained(stp), 1)
                    elif kind == "con" and stp[1] == 0:
                        act.wait_ge(filled(stp), nth(i, stp))
                        nc.scalar.activation(g1[:], bank(stp)[:], ACT.Identity, bias=R("b2")).then_inc(drained(stp), 1)
                    elif kind == "ffo":
                        act.wait_ge(drained(stp), after(i, stp))
                        nc.scalar.activation(th[:], f1[:], ACT.Tanh, scale=0.5).then_inc(th_made[1], 1)
                    elif kind == "av1" and stp[2] == 1:
                        g = stp[1]
                        act.wait_ge(filled("av1", g), nth(i, "av1", g))
                        copy(o1[:, g, :], bank("av1", g)[:]).then_inc(drained("av1", g), 1)
                    elif kind == "att":
                        act.wait_ge(filled(stp), nth(i, stp))
                        ps = bank(stp)
                        copy(att_t[:], ps[:]).then_inc(drained(stp), 1)

            trip_act(0, trips[0])
            with act.Fori(1, B) as i:
                trip_act(i, trips[1])
            trip_act(B, trips[2])

        @block.vector
        def _(dve):
            v = nc.vector

            dve.wait_ge(loads, 16 * 7)
            n = 0

            def setup(ins):
                nonlocal n
                n += 1
                ins.then_inc(setup_b, 1)
                dve.wait_ge(setup_b, n)

            def stg(name):
                return stage[:, STG[name][0]:STG[name][1]]

            def cut_weights(lead, rest, full):
                setup(v.tensor_copy(lead, full))
                setup(v.tensor_tensor(rest, full, lead.bitcast(F32), ALU.subtract))

            cut_weights(wq_lead[:].rearrange("p h n -> p (h n)"), wq_rest[:].rearrange("p h n -> p (h n)"), stg("wq"))
            cut_weights(qk_lead[:].rearrange("p a g n -> p (a g n)"), qk_rest[:].rearrange("p a g n -> p (a g n)"), stg("qk"))
            setup(v.tensor_copy(sel[:].rearrange("p h n -> p (h n)"), stg("sel")))
            setup(v.tensor_copy(spread[:].rearrange("p h n -> p (h n)"), stg("exp")))
            setup(v.tensor_copy(ident_b[:], ident))
            setup(v.tensor_copy(maskk_b[:], R("maskk")))
            null_row = stage2[:, ST2["null"][0]:ST2["null"][1]]
            for h in range(H):
                setup(v.tensor_tensor(gated0[:, 0:D0], stg("wq")[:, P * h:P * h + D0], null_row, ALU.mult))
                setup(v.tensor_reduce(R("vs")[:, D0 + h:D0 + h + 1], gated0[:, 0:D0], mybir.AxisListType.X, ALU.add))
            deq = stage[:, 0:3 * HID]
            setup(v.tensor_copy(deq, stage_i[:, 0:3 * HID]))
            setup(v.tensor_scalar(deq, deq, DEQ, None, ALU.mult))
            cut_weights(wgu_lead[:].rearrange("p a c n -> p (a c n)"), wgu_rest[:].rearrange("p a c n -> p (a c n)"), deq[:, 0:2 * HID])
            setup(v.tensor_scalar(wdown[:].rearrange("p c n -> p (c n)"), deq[:, 2 * HID:3 * HID], 0.5, None, ALU.mult))
            dve.wait_ge(setup_p, 1)
            setup(v.tensor_copy(null_out[:], banks[0][:, 0:P]))
            v.tensor_copy(gated0[:, 0:1], ident[:, 0:1]).then_inc(setup_v, 1)

            def trip_dve(i, trip):
                bank, filled, drained, nth, after, earlier = trip.bank, trip.filled, trip.drained, trip.nth, trip.after, trip.earlier
                chained = [iter(range(1, n + 1)) for n in CHAIN]

                def layer_norm(src, layer):
                    for n in range(NB):
                        last = v.bn_stats(stats[:, n, :], src[:, n, :])
                    last.then_inc(dve_chain[layer], 1)
                    dve.wait_ge(dve_chain[layer], count(i, dve_chain[layer], next(chained[layer])))
                    dve.sem_inc(passed, 1)
                    for n in range(NB):
                        last = v.bn_aggr(mv[:, n, :], stats[:, n, :])
                    last.then_inc(dve_chain[layer], 1)
                    dve.wait_ge(dve_chain[layer], count(i, dve_chain[layer], next(chained[layer])))
                    v.tensor_scalar(var_e[:], mv[:, :, 1], EPS, None, ALU.add).then_inc(var_made[layer], 1)
                    dve.wait_ge(rstd_made[layer], count(i, rstd_made[layer], 1))
                    for n in range(NB):
                        last = v.tensor_scalar(xn[:, n, :], src[:, n, :], mv[:, n, 0:1], rstd[:, n:n + 1], ALU.subtract, ALU.mult)
                    last.then_inc(xn_made[layer], 1)

                for stp in trip.steps:
                    kind = stp[0]
                    if kind == "ln":
                        if stp[1] == 0:
                            dve.wait_ge(x_loaded, count(i, x_loaded, 1))
                        other = ("xt", 1 - stp[1])
                        if trip.has(*other) and trip.steps.index(other) < trip.steps.index(stp):
                            dve.wait_ge(filled(other), nth(i, other))
                        layer_norm((x_t, x1_t)[stp[1]], stp[1])
                    elif kind == "xt":
                        dve.wait_ge(lead_made[stp[1]], count(i, lead_made[stp[1]], lead_of[stp]))
                        ps = bank(stp)
                        v.tensor_tensor(x_rest[stp[1]][:], ps[:], x_lead[stp[1]][:].bitcast(F32), ALU.subtract).then_inc(drained(stp), 1)
                    elif kind == "kv":
                        dve.wait_ge(lead_made[0], count(i, lead_made[0], lead_of[stp]))
                        ps = bank(stp)
                        v.tensor_tensor(k_rest[0:D0, :], ps[0:D0, :], k_lead[0:D0, :].bitcast(F32), ALU.subtract).then_inc(drained(stp), 1)
                    elif kind == "vs":
                        dve.wait_ge(filled(stp), nth(i, stp))
                        ps = bank(stp)[:].rearrange("p (n c) -> p n c", n=NB)
                        v.tensor_copy(v0[:], ps[:, :, 0:D0])
                        v.tensor_copy(s_null[:].rearrange("p h n -> p n h"), ps[:, :, D0:D0 + H]).then_inc(drained(stp), 1)
                    elif kind == "prep0":
                        h = stp[1]
                        dve.wait_ge(lead_made[0], count(i, lead_made[0], lead_of[stp]))
                        ps = bank(stp)
                        if h >= RING:
                            dve.wait_ge(drained("st", 0, h - RING, 2), after(i, "st", 0, h - RING, 2))
                            e = (h - RING) // 2
                            dve.wait_ge(q_top[e % 4], count(i, q_top[e % 4], e // 4 + 1))
                        v.tensor_tensor(q_two[:, h % RING, :], ps[:], cut[:, cut_at[stp], :].bitcast(F32), ALU.subtract).then_inc(drained(stp), 1)
                    elif kind == "prep1":
                        g = stp[1]
                        if g >= 2:
                            dve.wait_ge(drained("st", 1, GH * (g - 2) + 3, 2), after(i, "st", 1, GH * (g - 2) + 3, 2))
                        for n, (which, dst) in enumerate((("q", q1_st[:, g % 2, :]), ("k", k1_st[:]))):
                            dve.wait_ge(lead_made[1], count(i, lead_made[1], lead_of[stp] - 1 + n))
                            if g >= 1 and n == 1:
                                dve.wait_ge(k1_spread, count(i, k1_spread, GH * g))
                            v.scalar_tensor_tensor(dst, bank("prep1", which, g)[:], R("bqk")[:, NG * n + g:NG * n + g + 1],
                                                   cut1[:].bitcast(F32), ALU.add, ALU.subtract).then_inc(drained("prep1", which, g), 1)
                    elif kind == "sm":
                        layer, h, u = stp[1:]
                        dve.wait_ge(filled(stp), nth(i, stp))
                        ps = bank(stp)
                        dve.sem_inc(passed, 1)
                        for qb in ((3,), (2, 0), (1,))[u]:
                            w, at = P * (qb + 1), (384 if qb == 0 else 0)
                            last = v.tensor_tensor_reduce(ps[:, at:at + w], ps[:, at:at + w], R("maskq")[:, T - w:T], 1.0, -3e38,
                                                          ALU.add, ALU.max, rowmax[layer][:, h % GH, qb:qb + 1])
                        last.then_inc(drained(stp), 1)
                    elif kind == "max":
                        layer, g = stp[1:]
                        dve.wait_ge(drained("sm", layer, GH * g + 3, 2), after(i, "sm", layer, GH * g + 3, 2))
                        if layer == 0:
                            sn = s_null[:, GH * g:GH * g + GH, :]
                            v.tensor_tensor(rowmax[layer][:], rowmax[layer][:], sn, ALU.max).then_inc(dve_chain[layer], 1)
                            dve.wait_ge(dve_chain[layer], count(i, dve_chain[layer], next(chained[layer])))
                            mp = max_parts[0][:, g % 2, :].rearrange("p (e c h n) -> p c e (h n)", e=2, c=2, h=2)
                            lead, rest = mp[:, 0], mp[:, 1]
                        else:
                            mp = max_parts[1][:, g % 2, :].rearrange("p (h c n) -> p h c n", c=2, h=GH)
                            lead, rest = mp[:, :, 0], mp[:, :, 1]
                        if layer == 0:
                            v.tensor_tensor(p_arg[:, GH * g:GH * g + GH, :], sn, rowmax[layer][:], ALU.subtract).then_inc(p_arg_made, 1)
                        rows = rowmax[0][:].rearrange("p (e h) n -> p e (h n)", e=2) if layer == 0 else rowmax[1][:]
                        v.tensor_copy(lead.bitcast(F32R), rows).then_inc(dve_chain[layer], 1)
                        dve.wait_ge(dve_chain[layer], count(i, dve_chain[layer], next(chained[layer])))
                        v.tensor_tensor(rest, rows, lead, ALU.subtract).then_inc(parts_made[layer], 1)
                    elif kind == "gate":
                        dve.wait_ge(th_made[0], count(i, th_made[0], stp[1] + 1))
                        if stp[1] >= 1:
                            dve.wait_ge(drained("up", stp[1] - 1), after(i, "up", stp[1] - 1))
                        ps = bank(stp)
                        v.scalar_tensor_tensor(hg[:], th[:], 1.0, ps[:], ALU.add, ALU.mult).then_inc(drained(stp), 1)
                    elif kind == "up":
                        dve.wait_ge(filled(stp), nth(i, stp))
                        ps = bank(stp)
                        dve.wait_ge(drained("gate", stp[1]), after(i, "gate", stp[1]))
                        v.tensor_tensor(hidden[:, stp[1], :], ps[:], hg[:], ALU.mult).then_inc(drained(stp), 1)
                    elif kind == "down":
                        dve.wait_ge(th_made[0], count(i, th_made[0], NHID + 1))
                        ps = bank(stp)
                        v.scalar_tensor_tensor(gated0[:], th[:], 1.0, ps[:], ALU.add, ALU.mult).then_inc(drained(stp), 1)
                    elif kind == "lt":
                        dve.wait_ge(filled(stp), nth(i, stp))
                        ps = bank(stp)
                        d = ps[:].rearrange("p (n j c) -> p n j c", n=NB, j=GH)
                        for g in range(NG):
                            if g == NG - 1:
                                dve.wait_ge(p_null_made, count(i, p_null_made, 0))
                            last = v.tensor_copy(den_t[:, GH * g:GH * g + GH, :].rearrange("p h n -> p n h"), d[:, :, :, g])
                        last.then_inc(drained(stp), 1)
                        dve.wait_ge(drained(stp), after(i, stp))
                        v.tensor_tensor(den_t[:], den_t[:], p_null[:], ALU.add).then_inc(dve_chain[1], 1)
                        dve.wait_ge(dve_chain[1], count(i, dve_chain[1], next(chained[1])))
                        v.reciprocal(rec[:], den_t[:]).then_inc(dve_chain[1], 1)
                        dve.wait_ge(dve_chain[1], count(i, dve_chain[1], next(chained[1])))
                        rt = rt_in[:]
                        v.tensor_copy(rt[:, :, 0:H].bitcast(F32R), rec[:].rearrange("p h n -> p n h")).then_inc(dve_chain[1], 1)
                        dve.wait_ge(dve_chain[1], count(i, dve_chain[1], next(chained[1])))
                        v.tensor_tensor(rt[:, :, H:2 * H], rec[:].rearrange("p h n -> p n h"), rt[:, :, 0:H], ALU.subtract)
                        v.tensor_tensor(rt[:, :, 2 * H:3 * H], rec[:].rearrange("p h n -> p n h"),
                                                     p_null[:].rearrange("p h n -> p n h"), ALU.mult).then_inc(rt_made, 1)
                    elif kind == "norm":
                        dve.wait_ge(filled(stp), nth(i, stp))
                        ps = bank(stp)
                        v.tensor_tensor(o0[:, stp[1], :], ps[:], o0[:, stp[1], :], ALU.mult).then_inc(drained(stp), 1)
                    elif kind == "out0" and stp[1] == H // 2 - 1:
                        dve.wait_ge(filled("out0"), nth(i, "out0"))
                        v.scalar_tensor_tensor(gated0[:], gated0[:], 0.5, bank("out0")[:], ALU.mult,
                                               ALU.mult).then_inc(drained("out0"), 1)
                        dve.wait_ge(drained("out0"), after(i, "out0"))
                        dve.wait_ge(x_reloaded, count(i, x_reloaded, 1))
                        v.tensor_tensor(x1_t[:].rearrange("p n d -> p (n d)"), x1_t[:].rearrange("p n d -> p (n d)"), gated0[:],
                                        ALU.add).then_inc(x1_made, 1)
                        dve.wait_ge(x1_made, count(i, x1_made, 1))
                    elif kind == "v1":
                        dve.wait_ge(filled(stp), nth(i, stp))
                        ps = bank(stp)
                        for n in range(NB):
                            last = v.tensor_tensor(v1[:, n, 0:H * (D1 + 1)].rearrange("p (h c) -> p h c", h=H)[:, :, 0:D1], ps[:, P * n:P * n + P].rearrange("p (h d) -> p h d", h=H),
                                                   R("bv").rearrange("p (h d) -> p h d", h=H), ALU.add)
                        last.then_inc(drained(stp), 1)
                    elif kind == "s1":
                        dve.wait_ge(lead_made[1], count(i, lead_made[1], lead_of[stp]))
                        ps = bank(stp)
                        v.scalar_tensor_tensor(s_parts[M1:P, :], ps[M1:P, :], R("bin")[M1:P], s_parts[M1:P, :].bitcast(F32),
                                                     ALU.add, ALU.subtract).then_inc(drained(stp), 1)
                    elif kind == "con" and stp[1] == 1:
                        dve.wait_ge(filled(stp), nth(i, stp))
                        dve.wait_ge(drained("con", 0), after(i, "con", 0))
                        v.tensor_tensor(g1[:], bank(stp)[:], g1[:], ALU.add).then_inc(drained(stp), 1)
                    elif kind == "ffo":
                        dve.wait_ge(filled(stp), nth(i, stp))
                        for n in range(NB):
                            last = v.tensor_tensor(f1[:, P * n:P * n + P], bank(stp)[:, P * n:P * n + P], R("bout"), ALU.add)
                        last.then_inc(drained(stp), 1)
                        dve.wait_ge(th_made[1], count(i, th_made[1], 1))
                        v.scalar_tensor_tensor(f1[:], th[:], 1.0, f1[:], ALU.add, ALU.mult).then_inc(dve_chain[1], 1)
                        dve.wait_ge(dve_chain[1], count(i, dve_chain[1], next(chained[1])))
                    elif kind == "tr":
                        n = stp[1]
                        dve.wait_ge(filled(stp), nth(i, stp))
                        ps = bank(stp)[:].rearrange("p (g j c) -> p g j c", g=NG, j=GH)
                        v.reciprocal(rec1[:, n % 2, :].rearrange("p (g j) -> p g j", g=NG), ps[:, :, :, D1]).then_inc(dve_chain[1], 1)
                        dve.wait_ge(dve_chain[1], count(i, dve_chain[1], next(chained[1])))
                        a = att[:, n].rearrange("p (g j) d -> p g j d", g=NG)
                        for g in range(NG):
                            last = v.tensor_tensor(a[:, g], ps[:, g, :, 0:D1],
                                                   rec1[:, n % 2, GH * g:GH * g + GH].unsqueeze(2).broadcast_to([P, GH, D1]), ALU.mult)
                        last.then_inc(drained(stp), 1)
                    elif kind == "proj":
                        dve.wait_ge(filled(stp), nth(i, stp))
                        for n in range(NB):
                            last = v.tensor_tensor(att_t[:, P * n:P * n + P], bank(stp)[:, P * n:P * n + P], R("bp"), ALU.add)
                        last.then_inc(drained(stp), 1)
                        dve.wait_ge(drained(stp), after(i, stp))
                        v.scalar_tensor_tensor(f1[:], f1[:], 0.5, att_t[:], ALU.mult, ALU.mult).then_inc(dve_chain[1], 1)
                        dve.wait_ge(dve_chain[1], count(i, dve_chain[1], next(chained[1])))
                        v.tensor_tensor(x1_t[:].rearrange("p n d -> p (n d)"), x1_t[:].rearrange("p n d -> p (n d)"),
                                        f1[:], ALU.add).then_inc(out_made, 1)
                for half in range(2):
                    assert next(chained[half], None) is None or not trip.has("lt" if half else "gate"), half

            trip_dve(0, trips[0])
            with dve.Fori(1, B) as i:
                trip_dve(i, trips[1])
            trip_dve(B, trips[2])

        @block.tensor
        def _(pe):
            mm = nc.tensor.matmul

            pe.wait_ge(loads, 16 * 7)
            for p in range(H // 2):
                last = mm(banks[0][:, 0:P], stage2[:, P * p:P * p + P], wout[:, p, :], start=p == 0, stop=p == H // 2 - 1)
            last.then_inc(setup_p, 1)
            pe.wait_ge(setup_v, 1)
            pe.wait_ge(setup_g, 8)

            def trip_pe(i, trip):
                bank, filled, drained, nth, after, earlier = trip.bank, trip.filled, trip.drained, trip.nth, trip.after, trip.earlier
                def three(ps, w_lead, w_rest, x_l, x_r):
                    mm(ps, w_lead, x_l, start=True, stop=False)
                    mm(ps, w_rest, x_l, start=False, stop=False)
                    return mm(ps, w_lead, x_r, start=False, stop=True)

                for stp in trip.steps:
                    kind = stp[0]
                    if kind == "xt":
                        pe.wait_ge(xn_made[stp[1]], count(i, xn_made[stp[1]], 1))
                        pe.wait_ge(drained(stp), nth(i, stp))
                        ps = bank(stp)
                        for n in range(NB):
                            last = nc.tensor.transpose(ps[:, P * n:P * n + P], xn[:, n, :], ident)
                        last.then_inc(filled(stp), 1)
                    elif kind == "kv":
                        for name in trip.distinct(stp, ("xt", 0)):
                            pe.wait_ge(drained(name), after(i, name))
                        pe.wait_ge(drained(stp), nth(i, stp))
                        ps = bank(stp)
                        mm(ps[:], R("wkv"), xf[:], start=True, stop=True).then_inc(filled(stp), 1)
                    elif kind == "vs":
                        pe.wait_ge(drained(stp), nth(i, stp))
                        ps = bank(stp)
                        for n in range(NB):
                            last = mm(ps[:, P * n:P * n + P], xf[:, P * n:P * n + P], R("vs"), start=True, stop=True)
                        last.then_inc(filled(stp), 1)
                    elif kind == "prep0":
                        h = stp[1]
                        pe.wait_ge(drained(stp), nth(i, stp))
                        three(bank(stp)[:], wq_lead[:, h], wq_rest[:, h], x_lead[0][:], x_rest[0][:]).then_inc(filled(stp), 1)
                    elif kind == "prep1":
                        g = stp[1]
                        if g == 0:
                            for name in trip.distinct(("prep1", "q", g), ("xt", 1)):
                                pe.wait_ge(drained(name), after(i, name))
                        for n, which in enumerate("qk"):
                            name = ("prep1", which, g)
                            pe.wait_ge(drained(name), nth(i, name))
                            three(bank(name)[:], qk_lead[:, n, g], qk_rest[:, n, g], x_lead[1][:], x_rest[1][:]).then_inc(filled(name), 1)
                    elif kind == "sm":
                        layer, h, u = stp[1:]
                        if layer == 0:
                            for name in trip.distinct(None, ("kv",), ("prep0", h)):
                                pe.wait_ge(drained(name), after(i, name))
                            q, k = q_two[:, h % RING, :], k_lead[:]
                        else:
                            g, j = h // GH, h % GH
                            pe.wait_ge(drained("prep1", "q", g), after(i, "prep1", "q", g))
                            pe.wait_ge(k1_spread, count(i, k1_spread, GH * (g + 1)))
                            q, k = q1_st[:, g % 2, :], k1_head[:, h % (2 * GH), :]
                        pe.wait_ge(drained(stp), nth(i, stp))
                        ps = bank(stp)
                        for qb in ((3,), (2, 0), (1,))[u]:
                            w, at = P * (qb + 1), (384 if qb == 0 else 0)
                            last = mm(ps[:, at:at + w], q[:, P * qb:P * qb + P], k[:, 0:w], start=True, stop=True)
                        last.then_inc(filled(stp), 1)
                    elif kind == "mt":
                        layer, g = stp[1:]
                        pe.wait_ge(parts_made[layer], count(i, parts_made[layer], g + 1))
                        pe.wait_ge(drained(stp), nth(i, stp))
                        ps = bank(stp)
                        nc.tensor.transpose(ps[0:2 * GH * NB, 0:P], max_parts[layer][:, g % 2, :], ident).then_inc(filled(stp), 1)
                    elif kind == "st":
                        layer, h, u = stp[1:]
                        if layer == 0 and h % 2 == 0 and u == 0:
                            e = h // 2
                            pe.wait_ge(q_top[e % 4], count(i, q_top[e % 4], e // 4 + 1))
                        if h % GH == 0 and u == 0:
                            g = h // GH
                            if layer == 0:
                                pe.wait_ge(q_rows, count(i, q_rows, 2 * g + 2))
                            else:
                                pe.wait_ge(q1_rows, count(i, q1_rows, GH * (g + 1)))
                        pe.wait_ge(drained(stp), nth(i, stp))
                        ps = bank(stp)
                        for kb in ((0,), (1, 3), (2,))[u]:
                            at = KOFF[kb] % T
                            o = ps[:, at:at + kw(kb)]
                            ks, qs = slice(P * kb, P * kb + P), slice(P * kb, T)
                            mm(o[:, 0:P], maskk_b[:], ident_b[:], start=True, stop=False, skip_group_check=True)
                            if layer == 0:
                                mm(o, k_lead[:, ks], q_two[:, h % RING, qs], start=False, stop=False, skip_group_check=True)
                                last = mm(o, k_rest[:, ks], q_max[:, h % RING, qs], start=False, stop=True, skip_group_check=True)
                            else:
                                last = mm(o, k1_head[:, h % (2 * GH), ks], q1_st[:, (h // GH) % 2, qs], start=False, stop=True,
                                          skip_group_check=True)
                        last.then_inc(filled(stp), 1)
                    elif kind == "gate" or kind == "up":
                        n = 0 if kind == "gate" else 1
                        pe.wait_ge(drained(stp), nth(i, stp))
                        three(bank(stp)[:], wgu_lead[:, n, stp[1]], wgu_rest[:, n, stp[1]], x_lead[0][:], x_rest[0][:]).then_inc(filled(stp), 1)
                    elif kind == "down":
                        for name in trip.distinct(stp, ("up", NHID - 1)):
                            pe.wait_ge(drained(name), after(i, name))
                        pe.wait_ge(drained(stp), nth(i, stp))
                        ps = bank(stp)
                        for n in range(NB):
                            for c in range(NHID):
                                last = mm(ps[:, P * n:P * n + P], hidden[:, c, P * n:P * n + P], wdown[:, c], start=c == 0, stop=c == NHID - 1)
                        last.then_inc(filled(stp), 1)
                    elif kind == "av0":
                        p, part = stp[1:]
                        if p == 0 and part == 0:
                            for name in trip.distinct(("av0", p), ("vs",)):
                                pe.wait_ge(drained(name), after(i, name))
                        if part == 0:
                            pe.wait_ge(drained("st", 0, 2 * p + 1, 2), after(i, "st", 0, 2 * p + 1, 2))
                            pe.wait_ge(drained("av0", p), nth(i, "av0", p))
                        ps = bank("av0", p)
                        for kb in ((0, 3), (1, 2))[part]:
                            for c in range(2):
                                pr = probs[0][:, (2 * p + c) % GH, KOFF[kb]:KOFF[kb] + kw(kb)]
                                last = mm(ps[D0 * c:D0 * c + D0, P * kb:T], v0[:, kb, :], pr, start=kb == 0, stop=kb == 2,
                                          skip_group_check=True)
                        if part == 1:
                            last.then_inc(filled("av0", p), 1)
                    elif kind == "den":
                        g = stp[1]
                        if g == 0:
                            pe.wait_ge(drained("den"), nth(i, "den"))
                        ps = bank("den")
                        for kb in range(NB):
                            for j in range(GH):
                                pr = probs[0][:, j, KOFF[kb]:KOFF[kb] + kw(kb)]
                                last = mm(ps[32 * j:32 * j + 32, P * kb:T], R("onehot")[:, 32 * g:32 * g + 32], pr,
                                          start=kb == 0 and g == 0, stop=kb == NB - 1 and g == NG - 1, skip_group_check=True)
                        last.then_inc(probs_used, 1)
                        if g == NG - 1:
                            pe.wait_ge(probs_used, count(i, probs_used, NG))
                            pe.sem_inc(filled("den"), 1)
                    elif kind == "lt":
                        pe.wait_ge(bank_drained[7], earlier(i, 7))
                        pe.wait_ge(drained(stp), nth(i, stp))
                        ps = bank(stp)
                        for n in range(NB):
                            last = nc.tensor.transpose(ps[:, P * n:P * n + P], den_s[:, P * n:P * n + P], ident)
                        last.then_inc(filled(stp), 1)
                    elif kind == "rt":
                        pe.wait_ge(rt_made, count(i, rt_made, 1))
                        pe.wait_ge(drained(stp), nth(i, stp))
                        ps = bank(stp)
                        for n in range(NB):
                            last = nc.tensor.transpose(ps[:, P * n:P * n + P], rt_in[:, n, :], ident)
                        last.then_inc(filled(stp), 1)
                    elif kind == "norm":
                        if stp[1] == 0:
                            for name in trip.distinct(stp, ("rt",)):
                                pe.wait_ge(drained(name), after(i, name))
                        pe.wait_ge(drained(stp), nth(i, stp))
                        mm(bank(stp)[:], sel[:, stp[1]], rt_r[:], start=True, stop=True).then_inc(filled(stp), 1)
                    elif kind == "out0":
                        p = stp[1]
                        pe.wait_ge(drained("norm", p), after(i, "norm", p))
                        if p == 0:
                            pe.wait_ge(drained("out0"), nth(i, "out0"))
                        ps = bank("out0")
                        for n in range(NB):
                            c = slice(P * n, P * n + P)
                            last = mm(ps[:, c], o0[:, p, c], wout[:, p, :], start=p == 0 and n == 0, stop=False, skip_group_check=True)
                            if p == H // 2 - 1:
                                last = mm(ps[:, c], rt_f[:, c], null_out[:], start=False, stop=True, skip_group_check=True)
                        if p == H // 2 - 1:
                            last.then_inc(filled("out0"), 1)
                    elif kind == "v1":
                        pe.wait_ge(drained(stp), nth(i, stp))
                        ps = bank(stp)
                        for n in range(NB):
                            last = mm(ps[:, P * n:P * n + P], xf[:, P * n:P * n + P], R("wv"), start=True, stop=True)
                        last.then_inc(filled(stp), 1)
                    elif kind == "s1":
                        pe.wait_ge(drained(stp), nth(i, stp))
                        mm(bank(stp)[:], R("win"), xf[:], start=True, stop=True).then_inc(filled(stp), 1)
                    elif kind == "ex":
                        if stp[1] == 0:
                            for name in trip.distinct(stp, ("s1",)):
                                pe.wait_ge(drained(name), after(i, name))
                        pe.wait_ge(drained(stp), nth(i, stp))
                        mm(bank(stp)[:], spread[:, stp[1]], s_parts, start=True, stop=True).then_inc(filled(stp), 1)
                    elif kind == "con":
                        half = stp[1]
                        pe.wait_ge(drained(stp), nth(i, stp))
                        for name in trip.distinct(stp, ("ex", 4 * half + 2), ("ex", 4 * half + 3)):
                            pe.wait_ge(drained(name), after(i, name))
                        for n in range(4 * half, 4 * half + 4):
                            j = n % 4
                            last = mm(bank(stp)[32 * j:32 * j + 32, :], R("w2")[:, 32 * n:32 * n + 32], pieces[:, j, :],
                                      start=True, stop=True, skip_group_check=True)
                        last.then_inc(filled(stp), 1)
                    elif kind == "ffo":
                        for name in trip.distinct(stp, ("con", 1)):
                            pe.wait_ge(drained(name), after(i, name))
                        pe.wait_ge(drained(stp), nth(i, stp))
                        ps = bank(stp)
                        for n in range(NB):
                            last = mm(ps[:, P * n:P * n + P], g1[:, P * n:P * n + P], R("wo1"), start=True, stop=True)
                        last.then_inc(filled(stp), 1)
                    elif kind == "av1":
                        g, part = stp[1:]
                        if g == 0 and part == 0:
                            for name in trip.distinct(("av1", g), ("v1",)):
                                pe.wait_ge(drained(name), after(i, name))
                        if part == 0:
                            pe.wait_ge(drained("st", 1, GH * g + 3, 2), after(i, "st", 1, GH * g + 3, 2))
                            pe.wait_ge(drained("av1", g), nth(i, "av1", g))
                        ps = bank("av1", g)
                        for kb in ((0, 3), (1, 2))[part]:
                            for j in range(GH):
                                at = (D1 + 1) * (GH * g + j)
                                pr = probs[1][:, j, KOFF[kb]:KOFF[kb] + kw(kb)]
                                last = mm(ps[32 * j:32 * j + 32, P * kb:T], v1[:, kb, at:at + 32], pr, start=kb == 0, stop=kb == 2, skip_group_check=True)
                        if part == 1:
                            last.then_inc(filled("av1", g), 1)
                    elif kind == "tr":
                        n = stp[1]
                        if n == 0:
                            for name in trip.distinct(stp, ("av1", NG - 1)):
                                pe.wait_ge(drained(name), after(i, name))
                        pe.wait_ge(drained(stp), nth(i, stp))
                        ps = bank(stp)
                        for g in range(NG):
                            last = nc.tensor.transpose(ps[:, P * g:P * g + P], o1[:, g, P * n:P * n + P], ident)
                        last.then_inc(filled(stp), 1)
                    elif kind == "att":
                        for name in trip.distinct(stp, ("tr", NB - 2), ("tr", NB - 1)):
                            pe.wait_ge(drained(name), after(i, name))
                        pe.wait_ge(drained(stp), nth(i, stp))
                        ps = bank(stp)
                        for n in range(NB):
                            last = nc.tensor.transpose(ps[:, P * n:P * n + P], att[:, n].rearrange("p h d -> p (h d)"), ident)
                        last.then_inc(filled(stp), 1)
                    elif kind == "proj":
                        for name in trip.distinct(stp, ("att",)):
                            pe.wait_ge(drained(name), after(i, name))
                        pe.wait_ge(drained(stp), nth(i, stp))
                        ps = bank(stp)
                        for n in range(NB):
                            last = mm(ps[:, P * n:P * n + P], att_t[:, P * n:P * n + P], R("wp"), start=True, stop=True)
                        last.then_inc(filled(stp), 1)

            trip_pe(0, trips[0])
            with pe.Fori(1, B) as i:
                trip_pe(i, trips[1])
            trip_pe(B, trips[2])


def kernel(L0_attn_x, L0_attn_Wq, L0_attn_Wkv, L0_attn_null_kv, L0_attn_Wout, L0_ffn_w_gate, L0_ffn_w_up, L0_ffn_w_down,
           L1_attn_W_qkv, L1_attn_b_qkv, L1_attn_W_proj, L1_attn_b_proj, L1_ffn_Win, L1_ffn_bin_, L1_ffn_W1, L1_ffn_b1,
           L1_ffn_W2, L1_ffn_b2, L1_ffn_Wout, L1_ffn_bout):
    import concourse.bacc as bacc
    from concourse.bass_utils import run_bass_kernel_spmd

    f = np.float32
    a = lambda v: np.asarray(v)
    rows = lambda v: np.broadcast_to(a(v).reshape(1, -1), (P, a(v).size))
    part = np.arange(P)

    ident = np.eye(P, dtype=f)
    maskq = np.zeros((P, T), f)
    maskq[:, T - P:] = np.where(part[None, :] > part[:, None], f(NEG), f(0))
    maskk = np.where(part[None, :] > part[:, None], f(NEG), f(0)).astype(f)
    onehot = np.zeros((P, NG, 32), f)
    for g in range(NG):
        onehot[:, g, g::4] = 1
    lowmask = np.zeros((P, 3), f)
    lowmask[D0:, 0] = 1
    lowmask[part % 32 // D1 == 1, 1] = 1
    lowmask[part % 32 // D1 == 2, 2] = 1
    sel = np.zeros((P, H // 2, P), f)
    for h in range(H):
        sel[[h, H + h], h // 2, D0 * (h % 2):D0 * (h % 2) + D0] = 1
    spread = np.zeros((P, NE, P), f)
    for m in range(M1):
        c = IN1 * (m % (P // IN1))
        spread[[m, M1 + m], m // (P // IN1), c:c + IN1] = 1

    wq = a(L0_attn_Wq).reshape(D, H, 1, D0)
    wq2 = np.concatenate([wq, wq], axis=2).reshape(D, H * P)
    wkv = a(L0_attn_Wkv)
    vs = np.zeros((P, P), f)
    vs[:, 0:D0] = wkv
    nullsel = np.zeros((P, H // 2, P), f)
    for h in range(H):
        nullsel[D0 * (h % 2):D0 * (h % 2) + D0, h // 2, 2 * H + h] = a(L0_attn_null_kv)

    w3 = a(L1_attn_W_qkv).reshape(D, 3, NG, GH, D1)
    b3 = a(L1_attn_b_qkv).reshape(3, NG, GH, D1)
    qk = np.zeros((D, 2, NG, GH, 32), f)
    bqk = np.zeros((GH, 32, 2, NG), f)
    bqk_low = np.zeros((GH, 32, 2, NG), f)
    for n in range(2):
        for r in range(3):
            qk[:, n, :, :, D1 * r:D1 * r + D1] = w3[:, n]
            bqk[:, D1 * r:D1 * r + D1, n] = b3[n].transpose(1, 2, 0)
        bqk_low[:, D1 * (n + 1):D1 * (n + 2), n] = b3[n].transpose(1, 2, 0)
    bqk[:, 3 * D1:3 * D1 + 2, 1] = -1
    w2 = np.zeros((P, NE, 32), f)
    wo1 = np.zeros((P, D), f)
    b2 = np.zeros((P, 1), f)
    mt = P // IN1
    for m in range(M1):
        e, ml = m // mt, m % mt
        w2[IN1 * ml:IN1 * ml + IN1, e, mt * (e // 4) + ml] = a(L1_ffn_W2)[m]
        row = 32 * (e % 4) + mt * (e // 4) + ml
        wo1[row] = a(L1_ffn_Wout)[m]
        b2[row] = a(L1_ffn_b2)[m]
    two = lambda v: np.concatenate([v, v], axis=1)
    col = lambda v: a(v).reshape(NE, P).T
    packed = {
        "ident": ident, "wkv": two(wkv), "vs": vs, "maskq": maskq, "maskk": maskk, "onehot": onehot.reshape(P, -1),
        "lowmask": lowmask, "bqk": bqk.reshape(P, -1), "bqk_low": bqk_low.reshape(P, -1),
        "wv": a(L1_attn_W_qkv)[:, 2 * D:], "bv": rows(a(L1_attn_b_qkv)[2 * D:]), "wp": a(L1_attn_W_proj), "bp": rows(L1_attn_b_proj),
        "win": two(a(L1_ffn_Win)), "bin": two(a(L1_ffn_bin_).reshape(1, -1)).T, "w1": col(L1_ffn_W1), "b1": col(L1_ffn_b1),
        "w2": w2.reshape(P, -1), "b2": b2, "wo1": wo1, "bout": rows(L1_ffn_bout),
    }
    arrays = {
        "x": a(L0_attn_x),
        "res": np.ascontiguousarray(np.concatenate([packed[n] for n in RES], axis=1)),
        "stg": np.ascontiguousarray(np.concatenate([wq2, qk.reshape(D, -1), sel.reshape(P, -1), spread.reshape(P, -1)], axis=1)),
        "st2": np.ascontiguousarray(np.concatenate([nullsel.reshape(P, -1), rows(L0_attn_null_kv)], axis=1)),
        "wout": a(L0_attn_Wout),
        "wg": np.ascontiguousarray(a(L0_ffn_w_gate).T),
        "wu": np.ascontiguousarray(a(L0_ffn_w_up).T),
        "wd": np.ascontiguousarray(a(L0_ffn_w_down).T),
    }
    nc = bacc.Bacc("TRN2", target_bir_lowering=False, num_devices=1)
    aps = [nc.dram_tensor(f"{n}_dram", v.shape, mybir.dt.from_np(v.dtype), kind="ExternalInput").ap() for n, v in arrays.items()]
    out = nc.dram_tensor("out", (B, T, D), F32, kind="ExternalOutput").ap()
    two_layers(nc, *aps, out)
    r = run_bass_kernel_spmd(nc, [{f"{n}_dram": v for n, v in arrays.items()}], core_ids=[0])
    return r.results[0]["out"]
```

```python
from contextlib import ExitStack

import numpy as np

import concourse.bass as bass
from concourse import mybir

F32 = mybir.dt.float32
F32R = mybir.dt.float32r
BF16 = mybir.dt.bfloat16
I32 = mybir.dt.int32
ALU = mybir.AluOpType
ACT = mybir.ActivationFunctionType

P = 128
B, T, D = 16, 512, 128
NB = T // P
H = 16
NG = 4
GH = H // NG
D0 = 64
D1 = D // H
HID = 384
NHID = HID // P
M1, IN1 = 64, 16
NE = M1 * IN1 // P
EPS = 1e-5
CHAIN = (10, 15)
RING = 8
NEG = -1e30
DEQ = 1.0 / 127.0

RES = {}
_at = 0
for _name, _n in [("ident", P), ("wkv", P), ("vs", P), ("maskq", T), ("maskk", P), ("onehot", NG * 32), ("lowmask", 2),
                  ("bqk", 2 * NG), ("bqk_low", 2 * NG), ("wv", P), ("bv", P), ("wp", P), ("bp", P), ("win", P),
                  ("bin", 1), ("w1", NE), ("b1", NE), ("w2", NE * 32), ("b2", 1), ("wo1", P), ("bout", P)]:
    RES[_name] = (_at, _at + _n)
    _at += _n
NRES = _at
STG = {"wq": (0, 1024), "qk": (1024, 2048), "sel": (2048, 3072), "exp": (3072, 4096)}
NSTG = 4096
ST2 = {"nullsel": (0, 1024), "null": (1024, 1088)}
NST2 = 1088

KOFF = (0, 512, 1024, 896)


def kw(kb):
    return T - P * kb


ROOM = {"ln0": 2, "nx0": 1, "xt0": 2, "kv": 1, "vs": 1, "prep0": 2, "sm0": 0.42, "st0": 0.6, "gate": 1, "up": 1,
        "down": 3, "max0": 0.7, "mt0": 0.5, "av0": 1.2, "den": 0.88, "denc": 1, "lt": 3, "rt": 2.8, "norm": 2,
        "out0": 1, "ln1": 1.5, "nx1": 3, "xt1": 3, "prep1": 3, "v1": 2.4, "s1": 2, "ex": 1, "con": 1, "ffo": 2,
        "sm1": 0.6, "st1": 0.3, "max1": 0.6, "mt1": 1, "av1": 1, "tr": 1, "att": 2, "proj": 2}
UNTIL = 0.97


def room(stp):
    return ROOM[stp[0]] if stp[0] in ROOM else ROOM[f"{stp[0]}{stp[1]}"]


def units(layer, *heads):
    return [(kind, layer, h, u) for u in range(3) for kind, h in heads]


def spread_over(a, b, until):
    at = []
    for which, steps, end in ((0, a, 1), (1, b, until)):
        t, total = 0, sum(room(stp) for stp in steps)
        for stp in steps:
            at.append((t / total * end, which, len(at), stp))
            t += room(stp)
    return [stp for *_, stp in sorted(at)]


def first_half():
    s = [("ln", 0), ("nx", 0), ("xt", 0), ("kv",), ("prep0", 0), ("prep0", 1), ("vs",), ("gate", 0), ("up", 0)]
    s += units(0, ("sm", 0))
    s += units(0, ("sm", 1)) + [("gate", 1), ("up", 1)] + units(0, ("sm", 2)) + [("gate", 2)] + units(0, ("sm", 3))
    s += [("max", 0, 0), ("up", 2), ("prep0", 2), ("mt", 0, 0), ("down",)]
    for g in range(NG):
        h, p, more = GH * g, GH * g // 2, g + 1 < NG
        a = units(0, ("st", h), ("st", h + 1)) + [("av0", p, 0), ("av0", p, 1)] + units(0, ("st", h + 2), ("st", h + 3))
        if more:
            b = [("prep0", p + 3)] + units(0, ("sm", h + 4)) + units(0, ("sm", h + 5))
            a = spread_over(a, b + units(0, ("sm", h + 6)) + units(0, ("sm", h + 7)), 1) + [("max", 0, g + 1)]
        s += a + [("av0", p + 1, 0), ("av0", p + 1, 1)]
        if more:
            s += [("mt", 0, g + 1)]
        if g + 2 < NG:
            s += [("prep0", p + 4)]
        s += [("den", g)]
    return s + [("denc",)]


def second_half():
    s = [("lt",), ("rt",), ("norm", 0)]
    for p in range(1, H // 2):
        s += [("norm", p), ("out0", p - 1)]
    s += [("out0", H // 2 - 1), ("ln", 1), ("nx", 1), ("xt", 1)]
    s += [("prep1", 0), ("v1",), ("s1",), ("ex", 0), ("ex", 1)] + units(1, ("sm", 0))
    s += [("ex", 2), ("ex", 3)] + units(1, ("sm", 1)) + [("con", 0), ("ex", 4), ("ex", 5)]
    s += units(1, ("sm", 2)) + [("ex", 6), ("ex", 7)] + units(1, ("sm", 3))
    s += [("max", 1, 0), ("con", 1), ("mt", 1, 0), ("prep1", 1), ("ffo",)]
    for g in range(NG):
        h, n, more = GH * g, GH * g + GH, g + 1 < NG
        s += units(1, ("st", h))
        if more:
            s += units(1, ("st", h + 1), ("sm", n)) + units(1, ("st", h + 2), ("sm", n + 1), ("sm", n + 2))
            s += units(1, ("sm", n + 3))
            s += [("max", 1, g + 1)] + units(1, ("st", h + 3)) + [("mt", 1, g + 1)]
        else:
            s += units(1, ("st", h + 1)) + units(1, ("st", h + 2)) + units(1, ("st", h + 3))
        if g + 2 < NG:
            s += [("prep1", g + 2)]
        s += [("av1", g, 0), ("av1", g, 1)]
    return s + [("tr", n) for n in range(NB)] + [("att",), ("proj",)]


def merged(first, second):
    order = spread_over(first, second, UNTIL)
    kept = []
    while order:
        stp = order.pop(0)
        kept.append(stp)
        if stp[0] in ("av0", "av1") and stp[2] == 0:
            end = order.index(stp[:2] + (1,))
            beside, held = [], []
            for x in order[:end]:
                behind = any((x in second) == (y in second) for y in held)
                open_banks = sum(y[0] in ("st", "sm") for y in beside) < 6
                fits = x[0] in ("ln", "nx", "max", "out0", "den") or x[0] in ("st", "sm") and open_banks
                (beside if fits and not behind else held).append(x)
            order[:end + 1] = beside + [stp[:2] + (1,)] + held
    order = kept
    for one, other in ((("lt",), ("gate", 0)), (("out0", H // 2 - 1), ("down",)), (("out0", H // 2 - 1), ("den", 0)),
                       (("down",), ("ex", 0)), (("vs",), ("xt", 1)), (("xt", 0), ("nx", 1)), (("nx", 0), ("ln", 1)),
                       (("lt",), ("max", 0, 0)), (("proj",), ("denc",))):
        assert order.index(one) < order.index(other), (one, other)
    return order


SUMS = 7


def bank_plan(steps):
    uses, order = [0] * 8, {}
    turn = 0

    def take(name, bank=None):
        nonlocal turn
        if bank is None:
            bank, turn = turn % 7, turn + 1
        order[name] = (bank, uses[bank])
        uses[bank] += 1

    for st in steps:
        kind = st[0]
        if kind in ("st", "sm"):
            take(st)
        elif kind == "prep1":
            take(("prep1", "q", st[1]))
            take(("prep1", "k", st[1]))
        elif kind in ("den", "out0"):
            if st[1] == 0:
                take((kind,), SUMS)
        elif kind in ("av0", "av1"):
            if st[2] == 0:
                take(st[:2])
        elif kind not in ("ln", "nx", "max", "denc"):
            take(st)
    return order, uses


class Trip:

    def __init__(self, steps, full, banks, bank_filled, bank_drained):
        self.steps = steps
        self.unit, self.uses = bank_plan(steps)
        self.full, self.banks, self.bank_filled, self.bank_drained = full, banks, bank_filled, bank_drained
        self.missing = [0] * 8

    def _before(self, i, b):
        return 0 if isinstance(i, int) and i == 0 else i * self.full[b] - self.missing[b]

    def _plan(self, name):
        return self.unit[name[0] if isinstance(name[0], tuple) else name]

    def has(self, *name):
        return name in self.unit

    def bank(self, *name):
        return self.banks[self._plan(name)[0]]

    def filled(self, *name):
        return self.bank_filled[self._plan(name)[0]]

    def drained(self, *name):
        return self.bank_drained[self._plan(name)[0]]

    def nth(self, i, *name):
        b, k = self._plan(name)
        return self._before(i, b) + (k + 1)

    def after(self, i, *name):
        b, k = self._plan(name)
        return self._before(i, b) + (k + 2)

    def distinct(self, own, *names):
        last = {}
        for name in names:
            b, k = self.unit[name]
            if b != (self.unit[own][0] if own else None) and k >= self.unit[last.get(b, name)][1]:
                last[b] = name
        return last.values()

    def earlier(self, i, b):
        return self._before(i, b) + 1


def two_layers(nc, x_d, res_d, stg_d, st2_d, wout_d, wg_d, wu_d, wd_d, out_d):
    with ExitStack() as ctx:
        def sb(name, shape, dt=F32):
            return ctx.enter_context(nc.sbuf_tensor(name, shape, dt))

        def sem(name):
            return ctx.enter_context(nc.semaphore(name))

        res = sb("res", [P, NRES])
        wq_lead, wq_rest = sb("wq_lead", [P, H // 2, P], F32R), sb("wq_rest", [P, H // 2, P], F32R)
        wgu_lead, wgu_rest = sb("wgu_lead", [P, 2, NHID, P], F32R), sb("wgu_rest", [P, 2, NHID, P], F32R)
        qk_lead, qk_rest = sb("qk_lead", [P, 2, NG, P], F32R), sb("qk_rest", [P, 2, NG, P], F32R)
        sel = sb("sel", [P, H // 2, P], F32R)
        spread = sb("spread", [P, NE, P], F32R)
        wout = sb("wout", [P, H // 2, P])
        wdown = sb("wdown", [P, NHID, P])
        null_out = sb("null_out", [P, P])
        ident_b, maskk_b = sb("ident_b", [P, P], BF16), sb("maskk_b", [P, P], BF16)
        half_neg = sb("half_neg", [P, NB])

        x_t, xn = sb("x_t", [P, NB, D]), sb("xn", [P, NB, D])
        x1_t = sb("x1_t", [P, NB, D])
        stats, mv, var_e, rstd = sb("stats", [P, NB, 6]), sb("mv", [P, NB, 2]), sb("var_e", [P, NB]), sb("rstd", [P, NB])
        xf = sb("xf", [P, T])
        x_lead = sb("x0_lead", [P, T], F32R), sb("x1_lead", [P, T], F32R)
        x_rest = sb("x0_rest", [P, T], F32R), sb("x1_rest", [P, T], F32R)
        k_lead, k_rest = sb("k_lead", [P, T], F32R), sb("k_rest", [P, 2, T], F32R)
        v0, s_null = sb("v0", [P, NB, D0]), sb("s_null", [P, H, NB])
        q_rest, cut1 = sb("q_rest", [P, 2, T], F32R), sb("cut1", [P, T], F32R)
        q_two, q_max = sb("q_two", [P, RING, T], F32R), sb("q_max", [P, RING, T], F32R)
        q1_st, k1_st = sb("q1_st", [P, 2, T], F32R), sb("k1_st", [P, T], F32R)
        k1_head = sb("k1_head", [P, 2 * GH, T], F32R)
        o0, o1 = sb("o0", [P, H // 2, T]), sb("o1", [P, NG, T])
        probs = sb("probs0", [P, GH, 1280]), sb("probs1", [P, GH, 1280])
        v1 = sb("v1", [P, NB, H * (D1 + 1) + 32 - (D1 + 1)])
        rowmax = sb("rowmax0", [P, GH, NB]), sb("rowmax1", [P, GH, NB])
        max_parts = sb("max_parts0", [P, 2, 2 * GH * NB]), sb("max_parts1", [P, 2, 2 * GH * NB])
        max_t = sb("max_t0", [2 * GH * NB, 2, P], F32R), sb("max_t1", [2 * GH * NB, 2, P], F32R)
        p_arg, p_null = sb("p_arg", [P, H, NB]), sb("p_null", [P, H, NB])
        den_s = sb("den_s", [P, T])
        den_t, rec = sb("den_t", [P, H, NB]), sb("rec", [P, H, NB])
        rt_in = sb("rt_in", [P, NB, P])
        rt_r, rt_f = cut1, k1_st[:].bitcast(F32)
        gated0, f1 = sb("gated0", [P, T]), sb("f1", [P, T])
        hg, hidden, pieces = f1, o1[:, 0:NHID], o1
        th = att_t = den_s
        s_parts, att = cut1[:], xn[:].rearrange("p n (h d) -> p n h d", h=H)
        g1 = xf
        rec1 = sb("rec1", [P, 2, H])
        banks = [ctx.enter_context(nc.psum_tensor(f"bank{n}", [P, T], F32)) for n in range(8)]
        stage = probs[0][:].rearrange("p h c -> p (h c)")
        stage2 = o0[:].rearrange("p h c -> p (h c)")
        stage_i = o1[:].rearrange("p h c -> p (h c)").bitcast(I32)

        def R(name):
            return res[:, RES[name][0]:RES[name][1]]

        ident = R("ident")

        counts = {}

        def counting(name, per, half=0, step=1, base=0):
            s = sem(name)
            counts[s.name] = per, half, step, base
            return s

        def count(i, s, n):
            per, half, step, base = counts[s.name]
            return i * (per * step) + (n + base - half * per) * step

        bank_filled = [sem(f"bank{n}_filled") for n in range(8)]
        bank_drained = [sem(f"bank{n}_drained") for n in range(8)]
        x_loaded, x_reloaded = counting("x_loaded", 1, 0, 16), counting("x_reloaded", 1, 1, 16)
        out_stored = counting("out_stored", 1, 1, 16, 1)
        var_made = counting("var0_made", 1), counting("var1_made", 1, 1)
        rstd_made = counting("rstd0_made", 1), counting("rstd1_made", 1, 1)
        xn_made = counting("xn0_made", 1), counting("xn1_made", 1, 1)
        x1_made, out_made = counting("x1_made", 1, 1), counting("out_made", 1, 1)
        lead_made = counting("lead0_made", 2 + H // 2), counting("lead1_made", 2 + 2 * NG, 1)
        parts_made = counting("parts0_made", NG), counting("parts1_made", NG, 1)
        q_top = [counting(f"q_top{n}", 5 * H // 8, 0, 16) for n in range(4)]
        q_rows = counting("q_rows", H, 0, 16)
        q1_rows, k1_spread = counting("q1_rows", NG * GH, 1, 16), counting("k1_spread", H, 1, 16)
        p_arg_made, p_null_made = counting("p_arg_made", NG), counting("p_null_made", NG)
        probs_used = counting("probs_used", NG)
        rt_made = counting("rt_made", 1, 1)
        th_made = counting("th0_made", NHID + 1), counting("th1_made", 1, 1)
        dve_chain = counting("dve_chain0", CHAIN[0]), counting("dve_chain1", CHAIN[1], 1)
        passed = sem("passed")
        loads, setup_v, setup_p, setup_g, setup_b = sem("loads"), sem("setup_v"), sem("setup_p"), sem("setup_g"), sem("setup_b")

        first, second = first_half(), second_half()
        both = merged(first, second)
        full = bank_plan(both)[1]
        trips = [Trip(s, full, banks, bank_filled, bank_drained)
                 for s in (first, both, second)]
        for trip in trips:
            trip.missing = [n - k for n, k in zip(full, trips[0].uses)]

        lead_of = {}
        for half in (first, second):
            n = 0
            for stp in half:
                n += {"xt": 1, "kv": 1, "prep0": 1, "s1": 1, "prep1": 2}.get(stp[0], 0)
                lead_of[stp] = n

        block = ctx.enter_context(nc.Block())

        @block.sync
        def _(sp):
            sp.dma_start(res[:], res_d).then_inc(loads, 16)
            sp.dma_start(stage[:, 0:NSTG], stg_d).then_inc(loads, 16)
            sp.dma_start(stage2[:, 0:NST2], st2_d).then_inc(loads, 16)
            sp.dma_start(wout[:], wout_d.rearrange("(c p) n -> p c n", p=P)).then_inc(loads, 16)
            sp.dma_start(stage_i[:, 0:HID], wg_d).then_inc(loads, 16)
            sp.dma_start(stage_i[:, HID:2 * HID], wu_d).then_inc(loads, 16)
            sp.dma_start(stage_i[:, 2 * HID:3 * HID].rearrange("p (c n) -> p c n", c=NHID),
                         wd_d.rearrange("(c p) n -> p c n", p=P)).then_inc(loads, 16)
            xv = x_d.rearrange("b (n p) d -> b p n d", p=P)
            ov = out_d.rearrange("b (n p) d -> b p n d", p=P)
            sp.dma_start(x_t[:], xv[0]).then_inc(x_loaded, 16)
            def trip_sp(i, trip):
                bank, filled, drained, nth, after, earlier = trip.bank, trip.filled, trip.drained, trip.nth, trip.after, trip.earlier
                for stp in trip.steps:
                    kind = stp[0]
                    if kind == "xt" and stp[1] == 0:
                        sp.wait_ge(xn_made[0], count(i, xn_made[0], 1))
                        sp.sem_inc(passed, 1)
                        sp.dma_start(x_t[:], xv[(i + 1) % B]).then_inc(x_loaded, 16)
                    elif kind == "lt":
                        sp.wait_ge(out_stored, count(i, out_stored, 0))
                        sp.sem_inc(passed, 1)
                        sp.dma_start(x1_t[:], xv[i - 1]).then_inc(x_reloaded, 16)
                    elif kind == "prep0":
                        p = stp[1]
                        r, made = 2 * p % RING, q_top[p % 4]
                        rest = q_rest[:, p % 2, :].bitcast(F32)
                        up, low = slice(0, D0), slice(D0, P)
                        sp.wait_ge(lead_made[0], count(i, lead_made[0], lead_of[stp]))
                        sp.sem_inc(passed, 1)
                        sp.dma_start(q_two[up, r, :].bitcast(F32), q_max[up, r, :].bitcast(F32)).then_inc(made, 16)
                        sp.dma_start(q_two[low, r + 1, :].bitcast(F32), q_max[low, r, :].bitcast(F32)).then_inc(made, 16)
                        sp.wait_ge(drained(stp), after(i, stp))
                        sp.sem_inc(passed, 1)
                        sp.dma_start(q_two[low, r, :].bitcast(F32), rest[up]).then_inc(made, 16)
                        sp.dma_start(q_two[up, r + 1, :].bitcast(F32), rest[low]).then_inc(made, 16)
                        sp.dma_start(q_max[low, r + 1, :].bitcast(F32), q_max[low, r, :].bitcast(F32)).then_inc(made, 16)
                    elif kind == "mt":
                        layer, g = stp[1:]
                        src = max_t[layer][:, g % 2, :].bitcast(F32)
                        sp.wait_ge(drained(stp), after(i, stp))
                        sp.sem_inc(passed, 1)
                        if layer == 0:
                            for j in range(GH):
                                r, top = (GH * g + j) % RING, (0 if j % 2 else D0)
                                sp.dma_start(q_max[top:top + 2, r, :].bitcast(F32), src[8 * j:8 * j + 8]).then_inc(q_rows, 16)
                        else:
                            for j in range(GH):
                                sp.dma_start(q1_st[32 * j + 24:32 * j + 26, g % 2, :].bitcast(F32),
                                             src[8 * j:8 * j + 8]).then_inc(q1_rows, 16)
                    elif kind == "prep1":
                        g = stp[1]
                        sp.wait_ge(drained("prep1", "k", g), after(i, "prep1", "k", g))
                        sp.sem_inc(passed, 1)
                        if g >= 2:
                            sp.wait_ge(drained("st", 1, GH * (g - 2) + 3, 2), after(i, "st", 1, GH * (g - 2) + 3, 2))
                            sp.sem_inc(passed, 1)
                        for j in range(GH):
                            sp.dma_start(k1_head[32 * j:32 * j + 32, GH * (g % 2) + j, :].bitcast(F32),
                                         k1_st[32 * j:32 * j + 32, :].bitcast(F32)).then_inc(k1_spread, 16)
                    elif kind == "proj":
                        sp.wait_ge(out_made, count(i, out_made, 1))
                        sp.sem_inc(passed, 1)
                        sp.dma_start(ov[i - 1], x1_t[:]).then_inc(out_stored, 16)

            trip_sp(0, trips[0])
            with sp.Fori(1, B) as i:
                trip_sp(i, trips[1])
            trip_sp(B, trips[2])
            sp.wait_ge(out_stored, 16 * (B + 1))
            sp.wait_ge(x_loaded, 16 * (B + 1))

        @block.gpsimd
        def _(pool):
            ones = v1[:, :, 0:H * (D1 + 1)].rearrange("p n (h c) -> p n h c", h=H)[:, :, :, D1]
            for b in range(8):
                pool.sem_inc(bank_drained[b], 1)
            pool.sem_inc(out_stored, 16)
            nc.gpsimd.memset(half_neg[:], -0.5).then_inc(setup_g, 1)
            nc.gpsimd.memset(q_max[:].bitcast(F32), 0.0).then_inc(setup_g, 1)
            nc.gpsimd.memset(k1_head[:].bitcast(F32), 0.0).then_inc(setup_g, 1)
            nc.gpsimd.memset(k_rest[:].bitcast(F32), 0.0).then_inc(setup_g, 1)
            nc.gpsimd.memset(rt_in[:], 0.0).then_inc(setup_g, 1)
            nc.gpsimd.memset(v1[:], 0.0).then_inc(setup_g, 1)
            pool.wait_ge(setup_g, 6)
            nc.gpsimd.memset(k_rest[D0:D0 + 2, 0, :].bitcast(F32), -1.0).then_inc(setup_g, 1)
            pool.wait_ge(setup_g, 7)
            nc.gpsimd.memset(k_rest[0:2, 1, :].bitcast(F32), -1.0).then_inc(setup_g, 1)
            pool.wait_ge(setup_g, 8)
            nc.gpsimd.memset(ones, 1.0).then_inc(setup_g, 1)
            pool.wait_ge(setup_g, 9)
            def rstd_of(i, layer):
                pool.wait_ge(var_made[layer], count(i, var_made[layer], 1))
                nc.gpsimd.tensor_tensor(rstd[:], var_e[:], half_neg[:], ALU.pow).then_inc(rstd_made[layer], 1)

            order = [stp[1] for stp in both if stp[0] == "ln"]
            rstd_of(0, 0)
            with pool.Fori(1, B) as i:
                for layer in order:
                    rstd_of(i, layer)
            rstd_of(B, 1)

        @block.scalar
        def _(act):
            def copy(out, in_):
                return nc.scalar.activation(out, in_, ACT.Copy)

            act.wait_ge(loads, 16 * 7)
            act.wait_ge(setup_v, 1)
            act.wait_ge(setup_g, 9)
            def trip_act(i, trip):
                bank, filled, drained, nth, after, earlier = trip.bank, trip.filled, trip.drained, trip.nth, trip.after, trip.earlier
                for stp in trip.steps:
                    kind = stp[0]
                    if kind == "xt":
                        act.wait_ge(filled(stp), nth(i, stp))
                        ps = bank(stp)
                        copy(xf[:], ps[:])
                        copy(x_lead[stp[1]][:], ps[:]).then_inc(lead_made[stp[1]], 1)
                    elif kind == "kv":
                        act.wait_ge(filled(stp), nth(i, stp))
                        ps = bank(stp)
                        copy(k_lead[:], ps[:]).then_inc(lead_made[0], 1)
                    elif kind == "prep0":
                        act.wait_ge(filled(stp), nth(i, stp))
                        ps = bank(stp)
                        copy(q_max[:, 2 * stp[1] % RING, :], ps[:]).then_inc(lead_made[0], 1)
                    elif kind == "prep1":
                        g = stp[1]
                        for n, which in enumerate("qk"):
                            act.wait_ge(filled("prep1", which, g), nth(i, "prep1", which, g))
                            ps = bank("prep1", which, g)
                            if n == 1:
                                act.wait_ge(drained("prep1", "q", g), after(i, "prep1", "q", g))
                            elif g >= 1:
                                act.wait_ge(drained("prep1", "k", g - 1), after(i, "prep1", "k", g - 1))
                            nc.scalar.activation(cut1[:], ps[:], ACT.Identity,
                                                 scale=R("lowmask")[:, n:n + 1],
                                                 bias=R("bqk_low")[:, NG * n + g:NG * n + g + 1]).then_inc(lead_made[1], 1)
                    elif kind == "mt":
                        layer, g = stp[1:]
                        act.wait_ge(filled(stp), nth(i, stp))
                        ps = bank(stp)
                        copy(max_t[layer][:, g % 2, :], ps[0:2 * GH * NB, 0:P]).then_inc(drained(stp), 1)
                        if layer == 0:
                            if g == 0 and trip.has("lt"):
                                act.wait_ge(rt_made, count(i, rt_made, 1))
                            act.wait_ge(p_arg_made, count(i, p_arg_made, g + 1))
                            nc.scalar.activation(p_null[:, GH * g:GH * g + GH, :], p_arg[:, GH * g:GH * g + GH, :],
                                                                  ACT.Exp, scale=D0 ** -0.5).then_inc(p_null_made, 1)
                    elif kind == "st":
                        layer, h, u = stp[1:]
                        scale = float(D0 if layer == 0 else D1) ** -0.5
                        if layer == 0 and u == 0 and not (trip is trips[0] and h < GH):
                            act.wait_ge(probs_used, count(i, probs_used, h // GH))
                        elif layer == 1 and u == 0 and h >= GH:
                            act.wait_ge(filled("av1", h // GH - 1), nth(i, "av1", h // GH - 1))
                        pr = probs[layer][:, h % GH, :]
                        a, b = ((0, 512), (512, 1024), (1024, 1280))[u]
                        act.wait_ge(filled(stp), nth(i, stp))
                        ps = bank(stp)
                        nc.scalar.activation(pr[:, a:b], ps[:, 0:b - a], ACT.Exp, scale=scale).then_inc(drained(stp), 1)
                    elif kind == "gate":
                        act.wait_ge(filled(stp), nth(i, stp))
                        ps = bank(stp)
                        if stp[1] >= 1:
                            act.wait_ge(drained("gate", stp[1] - 1), after(i, "gate", stp[1] - 1))
                        nc.scalar.activation(th[:], ps[:], ACT.Tanh, scale=0.5).then_inc(th_made[0], 1)
                    elif kind == "down":
                        act.wait_ge(filled(stp), nth(i, stp))
                        ps = bank(stp)
                        nc.scalar.activation(th[:], ps[:], ACT.Tanh, scale=0.5).then_inc(th_made[0], 1)
                    elif kind == "av0" and stp[2] == 1:
                        p = stp[1]
                        act.wait_ge(filled("av0", p), nth(i, "av0", p))
                        copy(o0[:, p, :], bank("av0", p)[:]).then_inc(drained("av0", p), 1)
                    elif kind == "denc":
                        if trip.has("proj"):
                            act.wait_ge(out_made, count(i, out_made, 1))
                        act.wait_ge(filled("den"), nth(i, "den"))
                        ps = bank("den")
                        copy(den_s[:], ps[:]).then_inc(drained("den"), 1)
                    elif kind == "rt":
                        act.wait_ge(filled(stp), nth(i, stp))
                        ps = bank(stp)
                        copy(rt_r[:], ps[:])
                        copy(rt_f, ps[:]).then_inc(drained(stp), 1)
                    elif kind == "s1":
                        act.wait_ge(filled(stp), nth(i, stp))
                        ps = bank(stp)
                        act.wait_ge(drained("prep1", "k", 0), after(i, "prep1", "k", 0))
                        nc.scalar.activation(s_parts, ps[:], ACT.Identity, bias=R("bin")).then_inc(lead_made[1], 1)
                    elif kind == "ex":
                        n = stp[1]
                        act.wait_ge(filled(stp), nth(i, stp))
                        ps = bank(stp)
                        if n == GH:
                            act.wait_ge(filled("con", 0), nth(i, "con", 0))
                        nc.scalar.activation(pieces[:, n % GH, :], ps[:], ACT.Relu, scale=R("w1")[:, n:n + 1],
                                                   bias=R("b1")[:, n:n + 1]).then_inc(drained(stp), 1)
                    elif kind == "con" and stp[1] == 0:
                        act.wait_ge(filled(stp), nth(i, stp))
                        nc.scalar.activation(g1[:], bank(stp)[:], ACT.Identity, bias=R("b2")).then_inc(drained(stp), 1)
                    elif kind == "ffo":
                        act.wait_ge(drained(stp), after(i, stp))
                        nc.scalar.activation(th[:], f1[:], ACT.Tanh, scale=0.5).then_inc(th_made[1], 1)
                    elif kind == "av1" and stp[2] == 1:
                        g = stp[1]
                        act.wait_ge(filled("av1", g), nth(i, "av1", g))
                        copy(o1[:, g, :], bank("av1", g)[:]).then_inc(drained("av1", g), 1)
                    elif kind == "att":
                        act.wait_ge(filled(stp), nth(i, stp))
                        ps = bank(stp)
                        copy(att_t[:], ps[:]).then_inc(drained(stp), 1)

            trip_act(0, trips[0])
            with act.Fori(1, B) as i:
                trip_act(i, trips[1])
            trip_act(B, trips[2])

        @block.vector
        def _(dve):
            v = nc.vector

            dve.wait_ge(loads, 16 * 7)
            n = 0

            def setup(ins):
                nonlocal n
                n += 1
                ins.then_inc(setup_b, 1)
                dve.wait_ge(setup_b, n)

            def stg(name):
                return stage[:, STG[name][0]:STG[name][1]]

            def cut_weights(lead, rest, full):
                setup(v.tensor_copy(lead, full))
                setup(v.tensor_tensor(rest, full, lead.bitcast(F32), ALU.subtract))

            cut_weights(wq_lead[:].rearrange("p h n -> p (h n)"), wq_rest[:].rearrange("p h n -> p (h n)"), stg("wq"))
            cut_weights(qk_lead[:].rearrange("p a g n -> p (a g n)"), qk_rest[:].rearrange("p a g n -> p (a g n)"), stg("qk"))
            setup(v.tensor_copy(sel[:].rearrange("p h n -> p (h n)"), stg("sel")))
            setup(v.tensor_copy(spread[:].rearrange("p h n -> p (h n)"), stg("exp")))
            setup(v.tensor_copy(ident_b[:], ident))
            setup(v.tensor_copy(maskk_b[:], R("maskk")))
            null_row = stage2[:, ST2["null"][0]:ST2["null"][1]]
            for h in range(H):
                setup(v.tensor_tensor(gated0[:, 0:D0], stg("wq")[:, D0 * h:D0 * h + D0], null_row, ALU.mult))
                setup(v.tensor_reduce(R("vs")[:, D0 + h:D0 + h + 1], gated0[:, 0:D0], mybir.AxisListType.X, ALU.add))
            deq = stage[:, 0:3 * HID]
            setup(v.tensor_copy(deq, stage_i[:, 0:3 * HID]))
            setup(v.tensor_scalar(deq, deq, DEQ, None, ALU.mult))
            cut_weights(wgu_lead[:].rearrange("p a c n -> p (a c n)"), wgu_rest[:].rearrange("p a c n -> p (a c n)"),
                        deq[:, 0:2 * HID])
            setup(v.tensor_scalar(wdown[:].rearrange("p c n -> p (c n)"), deq[:, 2 * HID:3 * HID], 0.5, None, ALU.mult))
            dve.wait_ge(setup_p, 1)
            setup(v.tensor_copy(null_out[:], banks[0][:, 0:P]))
            v.tensor_copy(gated0[:, 0:1], ident[:, 0:1]).then_inc(setup_v, 1)

            def trip_dve(i, trip):
                bank, filled, drained, nth, after, earlier = trip.bank, trip.filled, trip.drained, trip.nth, trip.after, trip.earlier
                chained = [iter(range(1, n + 1)) for n in CHAIN]

                for stp in trip.steps:
                    kind = stp[0]
                    if kind == "ln":
                        if stp[1] == 0:
                            dve.wait_ge(x_loaded, count(i, x_loaded, 1))
                        layer = stp[1]
                        for n in range(NB):
                            last = v.bn_stats(stats[:, n, :], (x_t, x1_t)[layer][:, n, :])
                        last.then_inc(dve_chain[layer], 1)
                        dve.wait_ge(dve_chain[layer], count(i, dve_chain[layer], next(chained[layer])))
                        dve.sem_inc(passed, 1)
                        for n in range(NB):
                            last = v.bn_aggr(mv[:, n, :], stats[:, n, :])
                        last.then_inc(dve_chain[layer], 1)
                        dve.wait_ge(dve_chain[layer], count(i, dve_chain[layer], next(chained[layer])))
                        v.tensor_scalar(var_e[:], mv[:, :, 1], EPS, None, ALU.add).then_inc(var_made[layer], 1)
                    elif kind == "nx":
                        layer = stp[1]
                        dve.wait_ge(rstd_made[layer], count(i, rstd_made[layer], 1))
                        if layer == 1 and trip.has("xt", 0):
                            dve.wait_ge(filled("xt", 0), nth(i, "xt", 0))
                        for n in range(NB):
                            last = v.tensor_scalar(xn[:, n, :], (x_t, x1_t)[layer][:, n, :], mv[:, n, 0:1], rstd[:, n:n + 1],
                                                   ALU.subtract, ALU.mult)
                        last.then_inc(xn_made[layer], 1)
                    elif kind == "xt":
                        dve.wait_ge(lead_made[stp[1]], count(i, lead_made[stp[1]], lead_of[stp]))
                        ps = bank(stp)
                        v.tensor_tensor(x_rest[stp[1]][:], ps[:], x_lead[stp[1]][:].bitcast(F32),
                                        ALU.subtract).then_inc(drained(stp), 1)
                    elif kind == "kv":
                        dve.wait_ge(lead_made[0], count(i, lead_made[0], lead_of[stp]))
                        ps = bank(stp)
                        v.tensor_tensor(k_rest[0:D0, 0, :], ps[0:D0, :], k_lead[0:D0, :].bitcast(F32), ALU.subtract)
                        v.tensor_tensor(k_rest[D0:P, 1, :], ps[D0:P, :], k_lead[D0:P, :].bitcast(F32),
                                        ALU.subtract).then_inc(drained(stp), 1)
                    elif kind == "vs":
                        dve.wait_ge(filled(stp), nth(i, stp))
                        ps = bank(stp)[:].rearrange("p (n c) -> p n c", n=NB)
                        v.tensor_copy(v0[:], ps[:, :, 0:D0])
                        v.tensor_copy(s_null[:].rearrange("p h n -> p n h"), ps[:, :, D0:D0 + H]).then_inc(drained(stp), 1)
                    elif kind == "prep0":
                        p = stp[1]
                        dve.wait_ge(lead_made[0], count(i, lead_made[0], lead_of[stp]))
                        if p >= 2:
                            dve.wait_ge(q_top[p % 4 - 2], count(i, q_top[p % 4 - 2], 5 * ((p - 2) // 4 + 1)))
                        v.tensor_tensor(q_rest[:, p % 2, :], bank(stp)[:], q_max[:, 2 * p % RING, :].bitcast(F32),
                                        ALU.subtract).then_inc(drained(stp), 1)
                    elif kind == "prep1":
                        g = stp[1]
                        if g >= 2:
                            dve.wait_ge(drained("st", 1, GH * (g - 2) + 3, 2), after(i, "st", 1, GH * (g - 2) + 3, 2))
                        for n, (which, dst) in enumerate((("q", q1_st[:, g % 2, :]), ("k", k1_st[:]))):
                            dve.wait_ge(lead_made[1], count(i, lead_made[1], lead_of[stp] - 1 + n))
                            if g >= 1 and n == 1:
                                dve.wait_ge(k1_spread, count(i, k1_spread, GH * g))
                            v.scalar_tensor_tensor(dst, bank("prep1", which, g)[:], R("bqk")[:, NG * n + g:NG * n + g + 1],
                                                   cut1[:].bitcast(F32), ALU.add, ALU.subtract).then_inc(drained("prep1", which, g), 1)
                    elif kind == "sm":
                        layer, h, u = stp[1:]
                        dve.wait_ge(filled(stp), nth(i, stp))
                        ps = bank(stp)
                        dve.sem_inc(passed, 1)
                        for qb in ((3,), (2, 0), (1,))[u]:
                            w, at = P * (qb + 1), (P if qb == 2 else 0)
                            last = v.tensor_tensor_reduce(ps[:, at:at + w], ps[:, at:at + w], R("maskq")[:, T - w:T], 1.0, -3e38,
                                                          ALU.add, ALU.max, rowmax[layer][:, h % GH, qb:qb + 1])
                        last.then_inc(drained(stp), 1)
                    elif kind == "max":
                        layer, g = stp[1:]
                        dve.wait_ge(drained("sm", layer, GH * g + 3, 2), after(i, "sm", layer, GH * g + 3, 2))
                        if layer == 0:
                            sn = s_null[:, GH * g:GH * g + GH, :]
                            v.tensor_tensor(rowmax[layer][:], rowmax[layer][:], sn, ALU.max).then_inc(dve_chain[layer], 1)
                            dve.wait_ge(dve_chain[layer], count(i, dve_chain[layer], next(chained[layer])))
                            v.tensor_tensor(p_arg[:, GH * g:GH * g + GH, :], sn, rowmax[layer][:],
                                            ALU.subtract).then_inc(p_arg_made, 1)
                        mp = max_parts[layer][:, g % 2, :].rearrange("p (h c n) -> p h c n", c=2, h=GH)
                        lead, rest = mp[:, :, 0], mp[:, :, 1]
                        v.tensor_copy(lead.bitcast(F32R), rowmax[layer][:]).then_inc(dve_chain[layer], 1)
                        dve.wait_ge(dve_chain[layer], count(i, dve_chain[layer], next(chained[layer])))
                        v.tensor_tensor(rest, rowmax[layer][:], lead, ALU.subtract).then_inc(parts_made[layer], 1)
                    elif kind == "gate":
                        dve.wait_ge(th_made[0], count(i, th_made[0], stp[1] + 1))
                        if stp[1] >= 1:
                            dve.wait_ge(drained("up", stp[1] - 1), after(i, "up", stp[1] - 1))
                        ps = bank(stp)
                        v.scalar_tensor_tensor(hg[:], th[:], 1.0, ps[:], ALU.add, ALU.mult).then_inc(drained(stp), 1)
                    elif kind == "up":
                        dve.wait_ge(filled(stp), nth(i, stp))
                        ps = bank(stp)
                        dve.wait_ge(drained("gate", stp[1]), after(i, "gate", stp[1]))
                        v.tensor_tensor(hidden[:, stp[1], :], ps[:], hg[:], ALU.mult).then_inc(drained(stp), 1)
                    elif kind == "down":
                        dve.wait_ge(th_made[0], count(i, th_made[0], NHID + 1))
                        ps = bank(stp)
                        v.scalar_tensor_tensor(gated0[:], th[:], 1.0, ps[:], ALU.add, ALU.mult).then_inc(drained(stp), 1)
                    elif kind == "lt":
                        dve.wait_ge(filled(stp), nth(i, stp))
                        ps = bank(stp)
                        d = ps[:].rearrange("p (n j c) -> p n j c", n=NB, j=GH)
                        for g in range(NG):
                            if g == NG - 1:
                                dve.wait_ge(p_null_made, count(i, p_null_made, 0))
                            last = v.tensor_copy(den_t[:, GH * g:GH * g + GH, :].rearrange("p h n -> p n h"), d[:, :, :, g])
                        last.then_inc(drained(stp), 1)
                        dve.wait_ge(drained(stp), after(i, stp))
                        v.tensor_tensor(den_t[:], den_t[:], p_null[:], ALU.add).then_inc(dve_chain[1], 1)
                        dve.wait_ge(dve_chain[1], count(i, dve_chain[1], next(chained[1])))
                        v.reciprocal(rec[:], den_t[:]).then_inc(dve_chain[1], 1)
                        dve.wait_ge(dve_chain[1], count(i, dve_chain[1], next(chained[1])))
                        rt = rt_in[:]
                        v.tensor_copy(rt[:, :, 0:H].bitcast(F32R), rec[:].rearrange("p h n -> p n h")).then_inc(dve_chain[1], 1)
                        dve.wait_ge(dve_chain[1], count(i, dve_chain[1], next(chained[1])))
                        v.tensor_tensor(rt[:, :, H:2 * H], rec[:].rearrange("p h n -> p n h"), rt[:, :, 0:H], ALU.subtract)
                        v.tensor_tensor(rt[:, :, 2 * H:3 * H], rec[:].rearrange("p h n -> p n h"),
                                                     p_null[:].rearrange("p h n -> p n h"), ALU.mult).then_inc(rt_made, 1)
                    elif kind == "norm":
                        dve.wait_ge(filled(stp), nth(i, stp))
                        ps = bank(stp)
                        v.tensor_tensor(o0[:, stp[1], :], ps[:], o0[:, stp[1], :], ALU.mult).then_inc(drained(stp), 1)
                    elif kind == "out0" and stp[1] == H // 2 - 1:
                        dve.wait_ge(filled("out0"), nth(i, "out0"))
                        v.scalar_tensor_tensor(gated0[:], gated0[:], 0.5, bank("out0")[:], ALU.mult,
                                               ALU.mult).then_inc(drained("out0"), 1)
                        dve.wait_ge(drained("out0"), after(i, "out0"))
                        dve.wait_ge(x_reloaded, count(i, x_reloaded, 1))
                        v.tensor_tensor(x1_t[:].rearrange("p n d -> p (n d)"), x1_t[:].rearrange("p n d -> p (n d)"), gated0[:],
                                        ALU.add).then_inc(x1_made, 1)
                        dve.wait_ge(x1_made, count(i, x1_made, 1))
                    elif kind == "v1":
                        dve.wait_ge(filled(stp), nth(i, stp))
                        ps = bank(stp)
                        for n in range(NB):
                            last = v.tensor_tensor(v1[:, n, 0:H * (D1 + 1)].rearrange("p (h c) -> p h c", h=H)[:, :, 0:D1],
                                                   ps[:, P * n:P * n + P].rearrange("p (h d) -> p h d", h=H),
                                                   R("bv").rearrange("p (h d) -> p h d", h=H), ALU.add)
                        last.then_inc(drained(stp), 1)
                    elif kind == "s1":
                        dve.wait_ge(lead_made[1], count(i, lead_made[1], lead_of[stp]))
                        ps = bank(stp)
                        v.scalar_tensor_tensor(s_parts[M1:P, :], ps[M1:P, :], R("bin")[M1:P], s_parts[M1:P, :].bitcast(F32),
                                                     ALU.add, ALU.subtract).then_inc(drained(stp), 1)
                    elif kind == "con" and stp[1] == 1:
                        dve.wait_ge(filled(stp), nth(i, stp))
                        dve.wait_ge(drained("con", 0), after(i, "con", 0))
                        v.tensor_tensor(g1[:], bank(stp)[:], g1[:], ALU.add).then_inc(drained(stp), 1)
                    elif kind == "ffo":
                        dve.wait_ge(filled(stp), nth(i, stp))
                        for n in range(NB):
                            last = v.tensor_tensor(f1[:, P * n:P * n + P], bank(stp)[:, P * n:P * n + P], R("bout"), ALU.add)
                        last.then_inc(drained(stp), 1)
                        dve.wait_ge(th_made[1], count(i, th_made[1], 1))
                        v.scalar_tensor_tensor(f1[:], th[:], 1.0, f1[:], ALU.add, ALU.mult).then_inc(dve_chain[1], 1)
                        dve.wait_ge(dve_chain[1], count(i, dve_chain[1], next(chained[1])))
                    elif kind == "tr":
                        n = stp[1]
                        dve.wait_ge(filled(stp), nth(i, stp))
                        ps = bank(stp)[:].rearrange("p (g j c) -> p g j c", g=NG, j=GH)
                        v.reciprocal(rec1[:, n % 2, :].rearrange("p (g j) -> p g j", g=NG),
                                     ps[:, :, :, D1]).then_inc(dve_chain[1], 1)
                        dve.wait_ge(dve_chain[1], count(i, dve_chain[1], next(chained[1])))
                        a = att[:, n].rearrange("p (g j) d -> p g j d", g=NG)
                        for g in range(NG):
                            last = v.tensor_tensor(a[:, g], ps[:, g, :, 0:D1],
                                                   rec1[:, n % 2, GH * g:GH * g + GH].unsqueeze(2).broadcast_to([P, GH, D1]), ALU.mult)
                        last.then_inc(drained(stp), 1)
                    elif kind == "proj":
                        dve.wait_ge(filled(stp), nth(i, stp))
                        for n in range(NB):
                            last = v.tensor_tensor(att_t[:, P * n:P * n + P], bank(stp)[:, P * n:P * n + P], R("bp"), ALU.add)
                        last.then_inc(drained(stp), 1)
                        dve.wait_ge(drained(stp), after(i, stp))
                        v.scalar_tensor_tensor(f1[:], f1[:], 0.5, att_t[:], ALU.mult, ALU.mult).then_inc(dve_chain[1], 1)
                        dve.wait_ge(dve_chain[1], count(i, dve_chain[1], next(chained[1])))
                        v.tensor_tensor(x1_t[:].rearrange("p n d -> p (n d)"), x1_t[:].rearrange("p n d -> p (n d)"),
                                        f1[:], ALU.add).then_inc(out_made, 1)
                for half in range(2):
                    assert next(chained[half], None) is None or not trip.has("lt" if half else "gate"), half

            trip_dve(0, trips[0])
            with dve.Fori(1, B) as i:
                trip_dve(i, trips[1])
            trip_dve(B, trips[2])

        @block.tensor
        def _(pe):
            mm = nc.tensor.matmul

            pe.wait_ge(loads, 16 * 7)
            for p in range(H // 2):
                last = mm(banks[0][:, 0:P], stage2[:, P * p:P * p + P], wout[:, p, :], start=p == 0, stop=p == H // 2 - 1)
            last.then_inc(setup_p, 1)
            pe.wait_ge(setup_v, 1)
            pe.wait_ge(setup_g, 9)

            def trip_pe(i, trip):
                bank, filled, drained, nth, after, earlier = trip.bank, trip.filled, trip.drained, trip.nth, trip.after, trip.earlier
                def three(ps, w_lead, w_rest, x_l, x_r):
                    mm(ps, w_lead, x_l, start=True, stop=False)
                    mm(ps, w_rest, x_l, start=False, stop=False)
                    return mm(ps, w_lead, x_r, start=False, stop=True)

                for stp in trip.steps:
                    kind = stp[0]
                    if kind == "xt":
                        pe.wait_ge(xn_made[stp[1]], count(i, xn_made[stp[1]], 1))
                        pe.wait_ge(drained(stp), nth(i, stp))
                        ps = bank(stp)
                        for n in range(NB):
                            last = nc.tensor.transpose(ps[:, P * n:P * n + P], xn[:, n, :], ident)
                        last.then_inc(filled(stp), 1)
                    elif kind == "kv":
                        for name in trip.distinct(stp, ("xt", 0)):
                            pe.wait_ge(drained(name), after(i, name))
                        pe.wait_ge(drained(stp), nth(i, stp))
                        ps = bank(stp)
                        mm(ps[:], R("wkv"), xf[:], start=True, stop=True).then_inc(filled(stp), 1)
                    elif kind == "vs":
                        pe.wait_ge(drained(stp), nth(i, stp))
                        ps = bank(stp)
                        for n in range(NB):
                            last = mm(ps[:, P * n:P * n + P], xf[:, P * n:P * n + P], R("vs"), start=True, stop=True)
                        last.then_inc(filled(stp), 1)
                    elif kind == "prep0":
                        h = stp[1]
                        pe.wait_ge(drained(stp), nth(i, stp))
                        three(bank(stp)[:], wq_lead[:, h], wq_rest[:, h], x_lead[0][:], x_rest[0][:]).then_inc(filled(stp), 1)
                    elif kind == "prep1":
                        g = stp[1]
                        if g == 0:
                            for name in trip.distinct(("prep1", "q", g), ("xt", 1)):
                                pe.wait_ge(drained(name), after(i, name))
                        for n, which in enumerate("qk"):
                            name = ("prep1", which, g)
                            pe.wait_ge(drained(name), nth(i, name))
                            three(bank(name)[:], qk_lead[:, n, g], qk_rest[:, n, g], x_lead[1][:],
                                  x_rest[1][:]).then_inc(filled(name), 1)
                    elif kind == "sm":
                        layer, h, u = stp[1:]
                        if layer == 0:
                            if h == 0 and u == 0:
                                pe.wait_ge(drained("kv"), after(i, "kv"))
                            if h % 2 == 0 and u == 0:
                                p = h // 2
                                pe.wait_ge(q_top[p % 4], count(i, q_top[p % 4], 5 * (p // 4 + 1)))
                            q, k = q_two[:, h % RING, :], k_lead[:]
                        else:
                            g, j = h // GH, h % GH
                            pe.wait_ge(drained("prep1", "q", g), after(i, "prep1", "q", g))
                            pe.wait_ge(k1_spread, count(i, k1_spread, GH * (g + 1)))
                            q, k = q1_st[:, g % 2, :], k1_head[:, h % (2 * GH), :]
                        pe.wait_ge(drained(stp), nth(i, stp))
                        ps = bank(stp)
                        for qb in ((3,), (0, 2), (1,))[u]:
                            w, at = P * max(qb + 1, 2), (P if qb == 2 else 0)
                            last = mm(ps[:, at:at + w], q[:, P * qb:P * qb + P], k[:, 0:w], start=True, stop=True)
                        last.then_inc(filled(stp), 1)
                    elif kind == "mt":
                        layer, g = stp[1:]
                        pe.wait_ge(parts_made[layer], count(i, parts_made[layer], g + 1))
                        pe.wait_ge(drained(stp), nth(i, stp))
                        ps = bank(stp)
                        nc.tensor.transpose(ps[0:2 * GH * NB, 0:P], max_parts[layer][:, g % 2, :], ident).then_inc(filled(stp), 1)
                    elif kind == "st":
                        layer, h, u = stp[1:]
                        if h % GH == 0 and u == 0:
                            g = h // GH
                            if layer == 0:
                                pe.wait_ge(q_rows, count(i, q_rows, GH * (g + 1)))
                            else:
                                pe.wait_ge(q1_rows, count(i, q1_rows, GH * (g + 1)))
                        pe.wait_ge(drained(stp), nth(i, stp))
                        ps = bank(stp)
                        for kb in ((0,), (3, 1), (2,))[u]:
                            at = KOFF[kb] % T
                            o = ps[:, at:at + kw(kb)]
                            wide = P if kb == 3 else 0
                            ks, qs = slice(P * kb, P * kb + P), slice(P * kb - wide, T)
                            mm(o[:, 0:P], maskk_b[:], ident_b[:], start=True, stop=False, skip_group_check=True)
                            o = ps[:, at - wide:at + kw(kb)]
                            if layer == 0:
                                mm(o, k_lead[:, ks], q_two[:, h % RING, qs], start=False, stop=False, skip_group_check=True)
                                last = mm(o, k_rest[:, h % 2, ks], q_max[:, h % RING, qs], start=False, stop=True, skip_group_check=True)
                            else:
                                last = mm(o, k1_head[:, h % (2 * GH), ks], q1_st[:, (h // GH) % 2, qs], start=False, stop=True,
                                          skip_group_check=True)
                        last.then_inc(filled(stp), 1)
                    elif kind == "gate" or kind == "up":
                        n = 0 if kind == "gate" else 1
                        pe.wait_ge(drained(stp), nth(i, stp))
                        three(bank(stp)[:], wgu_lead[:, n, stp[1]], wgu_rest[:, n, stp[1]], x_lead[0][:],
                              x_rest[0][:]).then_inc(filled(stp), 1)
                    elif kind == "down":
                        for name in trip.distinct(stp, ("up", NHID - 1)):
                            pe.wait_ge(drained(name), after(i, name))
                        pe.wait_ge(drained(stp), nth(i, stp))
                        ps = bank(stp)
                        for n in range(NB):
                            for c in range(NHID):
                                last = mm(ps[:, P * n:P * n + P], hidden[:, c, P * n:P * n + P], wdown[:, c], start=c == 0,
                                          stop=c == NHID - 1)
                        last.then_inc(filled(stp), 1)
                    elif kind == "av0":
                        p, part = stp[1:]
                        if p == 0 and part == 0:
                            for name in trip.distinct(("av0", p), ("vs",)):
                                pe.wait_ge(drained(name), after(i, name))
                        if part == 0:
                            pe.wait_ge(drained("st", 0, 2 * p + 1, 2), after(i, "st", 0, 2 * p + 1, 2))
                            pe.wait_ge(drained("av0", p), nth(i, "av0", p))
                        ps = bank("av0", p)
                        for kb in ((0, 3), (1, 2))[part]:
                            for c in range(2):
                                pr = probs[0][:, (2 * p + c) % GH, KOFF[kb]:KOFF[kb] + kw(kb)]
                                last = mm(ps[D0 * c:D0 * c + D0, P * kb:T], v0[:, kb, :], pr, start=kb == 0, stop=kb == 2,
                                          skip_group_check=True)
                        if part == 1:
                            last.then_inc(filled("av0", p), 1)
                    elif kind == "den":
                        g = stp[1]
                        if g == 0:
                            pe.wait_ge(drained("den"), nth(i, "den"))
                        ps = bank("den")
                        for kb in range(NB):
                            for j in range(GH):
                                pr = probs[0][:, j, KOFF[kb]:KOFF[kb] + kw(kb)]
                                last = mm(ps[32 * j:32 * j + 32, P * kb:T], R("onehot")[:, 32 * g:32 * g + 32], pr,
                                          start=kb == 0 and g == 0, stop=kb == NB - 1 and g == NG - 1, skip_group_check=True)
                        last.then_inc(probs_used, 1)
                        if g == NG - 1:
                            pe.wait_ge(probs_used, count(i, probs_used, NG))
                            pe.sem_inc(filled("den"), 1)
                    elif kind == "lt":
                        pe.wait_ge(bank_drained[SUMS], earlier(i, SUMS))
                        pe.wait_ge(drained(stp), nth(i, stp))
                        ps = bank(stp)
                        for n in range(NB):
                            last = nc.tensor.transpose(ps[:, P * n:P * n + P], den_s[:, P * n:P * n + P], ident)
                        last.then_inc(filled(stp), 1)
                    elif kind == "rt":
                        pe.wait_ge(rt_made, count(i, rt_made, 1))
                        pe.wait_ge(drained(stp), nth(i, stp))
                        ps = bank(stp)
                        for n in range(NB):
                            last = nc.tensor.transpose(ps[:, P * n:P * n + P], rt_in[:, n, :], ident)
                        last.then_inc(filled(stp), 1)
                    elif kind == "norm":
                        if stp[1] == 0:
                            for name in trip.distinct(stp, ("rt",)):
                                pe.wait_ge(drained(name), after(i, name))
                        pe.wait_ge(drained(stp), nth(i, stp))
                        mm(bank(stp)[:], sel[:, stp[1]], rt_r[:], start=True, stop=True).then_inc(filled(stp), 1)
                    elif kind == "out0":
                        p = stp[1]
                        pe.wait_ge(drained("norm", p), after(i, "norm", p))
                        if p == 0:
                            pe.wait_ge(drained("out0"), nth(i, "out0"))
                        ps = bank("out0")
                        for n in range(NB):
                            c = slice(P * n, P * n + P)
                            last = mm(ps[:, c], o0[:, p, c], wout[:, p, :], start=p == 0 and n == 0, stop=False, skip_group_check=True)
                            if p == H // 2 - 1:
                                last = mm(ps[:, c], rt_f[:, c], null_out[:], start=False, stop=True, skip_group_check=True)
                        if p == H // 2 - 1:
                            last.then_inc(filled("out0"), 1)
                    elif kind == "v1":
                        pe.wait_ge(drained(stp), nth(i, stp))
                        ps = bank(stp)
                        for n in range(NB):
                            last = mm(ps[:, P * n:P * n + P], xf[:, P * n:P * n + P], R("wv"), start=True, stop=True)
                        last.then_inc(filled(stp), 1)
                    elif kind == "s1":
                        pe.wait_ge(drained(stp), nth(i, stp))
                        mm(bank(stp)[:], R("win"), xf[:], start=True, stop=True).then_inc(filled(stp), 1)
                    elif kind == "ex":
                        if stp[1] == 0:
                            for name in trip.distinct(stp, ("s1",)):
                                pe.wait_ge(drained(name), after(i, name))
                        pe.wait_ge(drained(stp), nth(i, stp))
                        mm(bank(stp)[:], spread[:, stp[1]], s_parts, start=True, stop=True).then_inc(filled(stp), 1)
                    elif kind == "con":
                        half = stp[1]
                        pe.wait_ge(drained(stp), nth(i, stp))
                        for name in trip.distinct(stp, ("ex", 4 * half + 2), ("ex", 4 * half + 3)):
                            pe.wait_ge(drained(name), after(i, name))
                        for n in range(4 * half, 4 * half + 4):
                            j = n % 4
                            last = mm(bank(stp)[32 * j:32 * j + 32, :], R("w2")[:, 32 * n:32 * n + 32], pieces[:, j, :],
                                      start=True, stop=True, skip_group_check=True)
                        last.then_inc(filled(stp), 1)
                    elif kind == "ffo":
                        for name in trip.distinct(stp, ("con", 1)):
                            pe.wait_ge(drained(name), after(i, name))
                        pe.wait_ge(drained(stp), nth(i, stp))
                        ps = bank(stp)
                        for n in range(NB):
                            last = mm(ps[:, P * n:P * n + P], g1[:, P * n:P * n + P], R("wo1"), start=True, stop=True)
                        last.then_inc(filled(stp), 1)
                    elif kind == "av1":
                        g, part = stp[1:]
                        if g == 0 and part == 0:
                            for name in trip.distinct(("av1", g), ("v1",)):
                                pe.wait_ge(drained(name), after(i, name))
                        if part == 0:
                            pe.wait_ge(drained("st", 1, GH * g + 3, 2), after(i, "st", 1, GH * g + 3, 2))
                            pe.wait_ge(drained("av1", g), nth(i, "av1", g))
                        ps = bank("av1", g)
                        for kb in ((0, 3), (1, 2))[part]:
                            for j in range(GH):
                                at = (D1 + 1) * (GH * g + j)
                                pr = probs[1][:, j, KOFF[kb]:KOFF[kb] + kw(kb)]
                                last = mm(ps[32 * j:32 * j + 32, P * kb:T], v1[:, kb, at:at + 32], pr, start=kb == 0,
                                          stop=kb == 2, skip_group_check=True)
                        if part == 1:
                            last.then_inc(filled("av1", g), 1)
                    elif kind == "tr":
                        n = stp[1]
                        if n == 0:
                            for name in trip.distinct(stp, ("av1", NG - 1)):
                                pe.wait_ge(drained(name), after(i, name))
                        pe.wait_ge(drained(stp), nth(i, stp))
                        ps = bank(stp)
                        for g in range(NG):
                            last = nc.tensor.transpose(ps[:, P * g:P * g + P], o1[:, g, P * n:P * n + P], ident)
                        last.then_inc(filled(stp), 1)
                    elif kind == "att":
                        for name in trip.distinct(stp, ("tr", NB - 2), ("tr", NB - 1)):
                            pe.wait_ge(drained(name), after(i, name))
                        pe.wait_ge(drained(stp), nth(i, stp))
                        ps = bank(stp)
                        for n in range(NB):
                            last = nc.tensor.transpose(ps[:, P * n:P * n + P], att[:, n].rearrange("p h d -> p (h d)"), ident)
                        last.then_inc(filled(stp), 1)
                    elif kind == "proj":
                        for name in trip.distinct(stp, ("att",)):
                            pe.wait_ge(drained(name), after(i, name))
                        pe.wait_ge(drained(stp), nth(i, stp))
                        ps = bank(stp)
                        for n in range(NB):
                            last = mm(ps[:, P * n:P * n + P], att_t[:, P * n:P * n + P], R("wp"), start=True, stop=True)
                        last.then_inc(filled(stp), 1)

            trip_pe(0, trips[0])
            with pe.Fori(1, B) as i:
                trip_pe(i, trips[1])
            trip_pe(B, trips[2])


def kernel(L0_attn_x, L0_attn_Wq, L0_attn_Wkv, L0_attn_null_kv, L0_attn_Wout, L0_ffn_w_gate, L0_ffn_w_up, L0_ffn_w_down,
           L1_attn_W_qkv, L1_attn_b_qkv, L1_attn_W_proj, L1_attn_b_proj, L1_ffn_Win, L1_ffn_bin_, L1_ffn_W1, L1_ffn_b1,
           L1_ffn_W2, L1_ffn_b2, L1_ffn_Wout, L1_ffn_bout):
    import concourse.bacc as bacc
    from concourse.bass_utils import run_bass_kernel_spmd

    f = np.float32
    a = lambda v: np.asarray(v)
    rows = lambda v: np.broadcast_to(a(v).reshape(1, -1), (P, a(v).size))
    part = np.arange(P)

    ident = np.eye(P, dtype=f)
    maskq = np.zeros((P, T), f)
    maskq[:, T - P:] = np.where(part[None, :] > part[:, None], f(NEG), f(0))
    maskk = np.where(part[None, :] > part[:, None], f(NEG), f(0)).astype(f)
    onehot = np.zeros((P, NG, 32), f)
    for g in range(NG):
        onehot[:, g, g::4] = 1
    lowmask = np.zeros((P, 2), f)
    lowmask[part % 32 // D1 == 1, 0] = 1
    lowmask[part % 32 // D1 == 2, 1] = 1
    sel = np.zeros((P, H // 2, P), f)
    for h in range(H):
        sel[[h, H + h], h // 2, D0 * (h % 2):D0 * (h % 2) + D0] = 1
    spread = np.zeros((P, NE, P), f)
    for m in range(M1):
        c = IN1 * (m % (P // IN1))
        spread[[m, M1 + m], m // (P // IN1), c:c + IN1] = 1

    wkv = a(L0_attn_Wkv)
    vs = np.zeros((P, P), f)
    vs[:, 0:D0] = wkv
    nullsel = np.zeros((P, H // 2, P), f)
    for h in range(H):
        nullsel[D0 * (h % 2):D0 * (h % 2) + D0, h // 2, 2 * H + h] = a(L0_attn_null_kv)

    w3 = a(L1_attn_W_qkv).reshape(D, 3, NG, GH, D1)
    b3 = a(L1_attn_b_qkv).reshape(3, NG, GH, D1)
    qk = np.zeros((D, 2, NG, GH, 32), f)
    bqk = np.zeros((GH, 32, 2, NG), f)
    bqk_low = np.zeros((GH, 32, 2, NG), f)
    for n in range(2):
        for r in range(3):
            qk[:, n, :, :, D1 * r:D1 * r + D1] = w3[:, n]
            bqk[:, D1 * r:D1 * r + D1, n] = b3[n].transpose(1, 2, 0)
        bqk_low[:, D1 * (n + 1):D1 * (n + 2), n] = b3[n].transpose(1, 2, 0)
    bqk[:, 3 * D1:3 * D1 + 2, 1] = -1
    w2 = np.zeros((P, NE, 32), f)
    wo1 = np.zeros((P, D), f)
    b2 = np.zeros((P, 1), f)
    mt = P // IN1
    for m in range(M1):
        e, ml = m // mt, m % mt
        w2[IN1 * ml:IN1 * ml + IN1, e, mt * (e // 4) + ml] = a(L1_ffn_W2)[m]
        row = 32 * (e % 4) + mt * (e // 4) + ml
        wo1[row] = a(L1_ffn_Wout)[m]
        b2[row] = a(L1_ffn_b2)[m]
    two = lambda v: np.concatenate([v, v], axis=1)
    col = lambda v: a(v).reshape(NE, P).T
    packed = {
        "ident": ident, "wkv": two(wkv), "vs": vs, "maskq": maskq, "maskk": maskk, "onehot": onehot.reshape(P, -1),
        "lowmask": lowmask, "bqk": bqk.reshape(P, -1), "bqk_low": bqk_low.reshape(P, -1),
        "wv": a(L1_attn_W_qkv)[:, 2 * D:], "bv": rows(a(L1_attn_b_qkv)[2 * D:]), "wp": a(L1_attn_W_proj), "bp": rows(L1_attn_b_proj),
        "win": two(a(L1_ffn_Win)), "bin": two(a(L1_ffn_bin_).reshape(1, -1)).T, "w1": col(L1_ffn_W1), "b1": col(L1_ffn_b1),
        "w2": w2.reshape(P, -1), "b2": b2, "wo1": wo1, "bout": rows(L1_ffn_bout),
    }
    arrays = {
        "x": a(L0_attn_x),
        "res": np.ascontiguousarray(np.concatenate([packed[n] for n in RES], axis=1)),
        "stg": np.ascontiguousarray(np.concatenate([a(L0_attn_Wq), qk.reshape(D, -1), sel.reshape(P, -1), spread.reshape(P, -1)], axis=1)),
        "st2": np.ascontiguousarray(np.concatenate([nullsel.reshape(P, -1), rows(L0_attn_null_kv)], axis=1)),
        "wout": a(L0_attn_Wout),
        "wg": np.ascontiguousarray(a(L0_ffn_w_gate).T),
        "wu": np.ascontiguousarray(a(L0_ffn_w_up).T),
        "wd": np.ascontiguousarray(a(L0_ffn_w_down).T),
    }
    nc = bacc.Bacc("TRN2", target_bir_lowering=False, num_devices=1)
    aps = [nc.dram_tensor(f"{n}_dram", v.shape, mybir.dt.from_np(v.dtype), kind="ExternalInput").ap() for n, v in arrays.items()]
    out = nc.dram_tensor("out", (B, T, D), F32, kind="ExternalOutput").ap()
    two_layers(nc, *aps, out)
    r = run_bass_kernel_spmd(nc, [{f"{n}_dram": v for n, v in arrays.items()}], core_ids=[0])
    return r.results[0]["out"]
```
